# Optimizing a Trainium2 kernel written in Bass

```python
import numpy as np
import jax
import jax.numpy as jnp

def _softmax(x, axis=-1):
    return jax.nn.softmax(x, axis=axis)

def _gelu(x):
    return jax.nn.gelu(x, approximate=True)

def _silu(x):
    return jax.nn.silu(x)

def _sigmoid(x):
    return jax.nn.sigmoid(x)

def _layernorm(x, axis=-1, eps=1e-05):
    m = jnp.mean(x, axis=axis, keepdims=True)
    v = jnp.var(x, axis=axis, keepdims=True)
    return (x - m) / jnp.sqrt(v + eps)

def _scatter_add(tgt, idx, src, axis=0):
    return tgt.at[idx].add(src)

def _segment_sum(src, seg, n):
    return jax.ops.segment_sum(src, seg, n)
kernel_name = 'mk_prb_d1_jaxref_r8_880fde'

def setup_inputs(seed: int=0):
    np.random.seed(seed)
    _w = jnp.asarray

    def _L0_attn_setup():
        import jax, jax.numpy as jnp
        import numpy as np
        N_HEADS = 16
        D_HEAD = 128
        D_MODEL = 256
        MAXLEN = 256
        key = jax.random.key(seed)
        ks = jax.random.split(key, 9)
        b, t = (2, 256)
        hd = N_HEADS * D_HEAD
        init = 0.02
        return {'x': jax.random.normal(ks[0], (b, t, D_MODEL), dtype=jnp.float32), 'Wq': jax.random.normal(ks[1], (D_MODEL, hd), dtype=jnp.float32) * init, 'bq': jnp.zeros((hd,), dtype=jnp.float32), 'Wk': jax.random.normal(ks[2], (D_MODEL, hd), dtype=jnp.float32) * init, 'bk': jnp.zeros((hd,), dtype=jnp.float32), 'Wv': jax.random.normal(ks[3], (D_MODEL, hd), dtype=jnp.float32) * init, 'bv': jnp.zeros((hd,), dtype=jnp.float32), 'Wo': jax.random.normal(ks[4], (hd, D_MODEL), dtype=jnp.float32) * init, 'bo': jnp.zeros((D_MODEL,), dtype=jnp.float32)}
    _L0_attn_in = _L0_attn_setup()

    def _L0_ffn_setup():
        import jax, jax.numpy as jnp
        import numpy as np
        TOPK = 6
        CAP = 128
        ROUTE_SCALE = 1.0
        key = jax.random.key(seed)
        k = jax.random.split(key, 6)
        B, T, C = (2, 256, 256)
        E, H, HS = (64, 32, 64)
        std = 0.01
        return {'x': jax.random.normal(k[0], (B, T, C), jnp.float32), 'w_gate': jax.random.normal(k[1], (C, E), jnp.float32) * std, 'w_shared_up': jax.random.normal(k[2], (C, 2 * HS), jnp.float32) * std, 'w_shared_down': jax.random.normal(k[3], (HS, C), jnp.float32) * std, 'w_up': jax.random.normal(k[4], (E, C, 2 * H), jnp.float32) * std, 'w_down': jax.random.normal(k[5], (E, H, C), jnp.float32) * std}
    _L0_ffn_in = _L0_ffn_setup()
    _d = {'L0_attn_x': _L0_attn_in['x'], 'L0_attn_Wq': _L0_attn_in['Wq'], 'L0_attn_bq': _L0_attn_in['bq'], 'L0_attn_Wk': _L0_attn_in['Wk'], 'L0_attn_bk': _L0_attn_in['bk'], 'L0_attn_Wv': _L0_attn_in['Wv'], 'L0_attn_bv': _L0_attn_in['bv'], 'L0_attn_Wo': _L0_attn_in['Wo'], 'L0_attn_bo': _L0_attn_in['bo'], 'L0_ffn_w_gate': _L0_ffn_in['w_gate'], 'L0_ffn_w_shared_up': _L0_ffn_in['w_shared_up'], 'L0_ffn_w_shared_down': _L0_ffn_in['w_shared_down'], 'L0_ffn_w_up': _L0_ffn_in['w_up'], 'L0_ffn_w_down': _L0_ffn_in['w_down']}
    _x0 = _d['L0_attn_x']
    _d['L0_attn_x'] = jax.random.normal(jax.random.fold_in(jax.random.key(seed), 1), (4, 1024, 256), dtype=_x0.dtype)
    del _x0
    return _d

def reference(L0_attn_x, L0_attn_Wq, L0_attn_bq, L0_attn_Wk, L0_attn_bk, L0_attn_Wv, L0_attn_bv, L0_attn_Wo, L0_attn_bo, L0_ffn_w_gate, L0_ffn_w_shared_up, L0_ffn_w_shared_down, L0_ffn_w_up, L0_ffn_w_down):

    def _L0_attn_ref(x, Wq, bq, Wk, bk, Wv, bv, Wo, bo):
        import jax, jax.numpy as jnp
        import numpy as np
        N_HEADS = 16
        D_HEAD = 128
        D_MODEL = 256
        MAXLEN = 256
        b, t, _ = x.shape
        h, dh = (N_HEADS, D_HEAD)
        scale = 1.0 / np.sqrt(dh).astype(np.float32)
        q = (x @ Wq + bq).reshape(b, h, t, dh)
        k = (x @ Wk + bk).reshape(b, t, h, dh).transpose(0, 2, 3, 1)
        v = (x @ Wv + bv).reshape(b, t, h, dh).transpose(0, 2, 1, 3)
        logits = jnp.einsum('bhtd,bhds->bhts', q, k) * scale
        mask = jnp.triu(jnp.full((t, t), -jnp.inf, dtype=x.dtype), k=1)
        weights = jax.nn.softmax(logits + mask, axis=-1)
        out = jnp.einsum('bhts,bhsd->bhtd', weights, v)
        out = out.transpose(0, 2, 1, 3).reshape(b, t, h * dh)
        return out @ Wo + bo

    def _L0_ffn_ref(x, w_gate, w_shared_up, w_shared_down, w_up, w_down):
        import jax, jax.numpy as jnp
        import numpy as np
        TOPK = 6
        CAP = 128
        ROUTE_SCALE = 1.0
        B, T, C = x.shape
        E = w_gate.shape[1]
        x_flat = x.reshape(-1, C)
        N = x_flat.shape[0]
        su = x_flat @ w_shared_up
        y_s, g_s = jnp.split(su, 2, axis=-1)
        shared = jax.nn.silu(g_s) * y_s @ w_shared_down
        scores = jax.nn.sigmoid(x_flat @ w_gate)
        _, topk_idx = jax.lax.top_k(scores, TOPK)
        w = jnp.take_along_axis(scores, topk_idx, axis=-1)
        w = w / w.sum(-1, keepdims=True) * ROUTE_SCALE
        flat_e = topk_idx.reshape(-1)
        oh = jax.nn.one_hot(flat_e, E, dtype=jnp.int32)
        pos = jnp.take_along_axis(jnp.cumsum(oh, axis=0), flat_e[:, None], axis=1)[:, 0] - 1
        valid = pos < CAP
        pos_c = jnp.where(valid, pos, CAP - 1)
        token_ids = jnp.repeat(jnp.arange(N), TOPK)
        x_disp = jnp.zeros((E, CAP, C), x.dtype).at[flat_e, pos].set(x_flat[token_ids], mode='drop')
        up = jnp.einsum('ecd,edh->ech', x_disp, w_up)
        g_r, v_r = jnp.split(up, 2, axis=-1)
        h_r = jax.nn.silu(g_r) * v_r
        out_r = jnp.einsum('ech,ehd->ecd', h_r, w_down)
        y_ts = out_r[flat_e, pos_c]
        y_ts = jnp.where(valid[:, None], y_ts, 0.0)
        routed = (y_ts.reshape(N, TOPK, C) * w[:, :, None]).sum(axis=1)
        return (shared + routed).reshape(B, T, C)
    x = L0_attn_x
    xn = _layernorm(x, axis=-1)
    x = x + _L0_attn_ref(xn, L0_attn_Wq, L0_attn_bq, L0_attn_Wk, L0_attn_bk, L0_attn_Wv, L0_attn_bv, L0_attn_Wo, L0_attn_bo) + _L0_ffn_ref(xn, L0_ffn_w_gate, L0_ffn_w_shared_up, L0_ffn_w_shared_down, L0_ffn_w_up, L0_ffn_w_down)
    return x

_drawn_inputs = setup_inputs


def setup_inputs(seed=0):
    import zlib

    import numpy as np

    out = dict(_drawn_inputs(seed))
    spreads = {'L0_attn_bq': (0.0, 0.8),
     'L0_attn_bk': (0.0, 0.8),
     'L0_attn_bv': (0.0, 0.1),
     'L0_attn_bo': (0.0, 0.1)}
    factors = {'L0_attn_Wq': 8.0,
     'L0_attn_Wk': 8.0,
     'L0_ffn_w_gate': 8.0,
     'L0_ffn_w_shared_up': 8.0,
     'L0_ffn_w_shared_down': 8.0,
     'L0_ffn_w_up': 8.0,
     'L0_ffn_w_down': 8.0}
    for name, (base, spread) in spreads.items():
        noise = np.random.default_rng([zlib.crc32(name.encode()), seed]).standard_normal(out[name].shape)
        drawn = base * np.exp(spread * noise) if base else spread * noise
        out[name] = jnp.asarray(drawn.astype(out[name].dtype))
    for name, factor in factors.items():
        out[name] = (out[name] * factor).astype(out[name].dtype)
    return out
```

```python
from contextlib import ExitStack

import concourse.bass as bass
from concourse import mybir

F32 = mybir.dt.float32
BF16 = mybir.dt.bfloat16
U32 = mybir.dt.uint32
ALU = mybir.AluOpType
ACT = mybir.ActivationFunctionType
AX = mybir.AxisListType

P = 128
TOPK = 6
CAP = 128
EPS = 1e-5
MASKED = -3.0e38
LOGIT_LOW, LOGIT_HIGH = -104.0, 16.7


def causal_attention_with_moe(nc, x, Wq, bq, Wk, bk, Wv, bv, Wo, bo, w_gate, w_sup, w_sdown, w_up, w_down, out):
    B, T, C = x.shape
    HD = Wq.shape[1]
    D = 128
    H = HD // D
    SCALE = float(D) ** -0.5
    KC = C // P
    NT = B * T // P
    TB = T // P
    TPH = T // H
    E = w_gate.shape[1]
    HE = w_down.shape[1]
    HS = w_sdown.shape[0]
    G4 = 4
    NG = NT // G4
    EG = 4
    SLOTS = E * CAP
    assert C == 256 and T == 1024 and H == 16 and E == 64 and EG * HE == P and H * D == HD

    xn_d = nc.dram_tensor("xn_rows", (NT * P, C), F32, kind="Internal").ap()
    xnT_d = nc.dram_tensor("xn_columns", (P, KC, NT * P), F32, kind="Internal").ap()
    disp_d = nc.dram_tensor("dispatched", (SLOTS, C), F32, kind="Internal").ap()
    eout_d = nc.dram_tensor("expert_out", (SLOTS + P, C), F32, kind="Internal").ap()

    x_v = x.rearrange("b (t p) c -> p (b t) c", p=P)
    out_v = out.rearrange("b (t p) c -> p (b t) c", p=P)
    wup_v = w_up.rearrange("(g e) (k p) n -> g p e k n", e=EG, p=P)
    wdn_v = w_down.rearrange("(g e) h c -> g (e h) c", e=EG)

    with ExitStack() as ctx:
        def sb(name, shape, dt=F32):
            return ctx.enter_context(nc.sbuf_tensor(name, shape, dt))

        def sem(name):
            return ctx.enter_context(nc.semaphore(name))

        ctx.enter_context(nc.allow_non_contiguous_dma("small bias columns and weight slices"))

        resid = sb("resid", [P, NT, C])
        routed = sb("routed", [P, NT, C])
        cvec = sb("cvec", [P, C])
        ident = sb("ident", [P, P])
        wq = sb("wq", [P, KC, HD])
        wo = sb("wo", [P, H, C])
        bqs = sb("bqs", [P, H])
        bkT = sb("bkT", [P, H])
        causal = sb("causal", [P, P])
        slot_idx = sb("slot_idx", [P, NT, TOPK], U32)
        gate_w = sb("gate_w", [P, NT, TOPK])

        xT = sb("xT", [P, KC, T])
        wkh = sb("wkh", [P, KC, D])
        wvh = sb("wvh", [P, KC, D])
        qT = sb("qT", [P, T])
        kT = sb("kT", [P, T])
        vh = sb("vh", [P, TB, D])
        prob = sb("prob", [P, 2, T])
        probT = sb("probT", [P, 2, T])
        oT = sb("oT", [P, 2, P])
        nmax = sb("nmax", [P, TB])
        rsum = sb("rsum", [P, TB])
        rinv = sb("rinv", [P, TB])
        hold_v = sb("hold_v", [P, 1])
        hold_p = sb("hold_p", [P, 2])

        ps_s = ctx.enter_context(nc.psum_tensor("ps_s", [P, 2, 2 * 512], F32))
        ps_t = ctx.enter_context(nc.psum_tensor("ps_t", [P, 2, 512], F32))
        ps_o = ctx.enter_context(nc.psum_tensor("ps_o", [P, 512], F32))
        ps_y = ctx.enter_context(nc.psum_tensor("ps_y", [P, 512], F32))

        x_in = sem("x_in")
        w_in = sem("w_in")
        const_ready = sem("const_ready")
        bias_ready = sem("bias_ready")
        fill_ready = sem("fill_ready")
        held = sem("held")
        stats_ready = sem("stats_ready")
        std_ready = sem("std_ready")
        ln_step = sem("ln_step")
        cvec_done = sem("cvec_done")
        cvec_ready = sem("cvec_ready")
        xn_ready = sem("xn_ready")
        xn_stored = sem("xn_stored")
        xt_done = sem("xt_done")
        xt_ready = sem("xt_ready")
        xt_stored = sem("xt_stored")
        g_done = sem("g_done")
        g_exp = sem("g_exp")
        z_step = sem("z_step")
        top_step = sem("top_step")
        z_read = sem("z_read")
        hs_step = sem("hs_step")
        hs_ready = sem("hs_ready")
        ht_done = sem("ht_done")
        ht_ready = sem("ht_ready")
        d_done = sem("d_done")
        d_added = sem("d_added")
        route_step = sem("route_step")
        mask_ready = sem("mask_ready")
        count_done = sem("count_done")
        logit_exp = sem("logit_exp")
        route_ready = sem("route_ready")
        zero_stored = sem("zero_stored")

        xT_in = sem("xT_in")
        wkv_in = sem("wkv_in")
        q_done = sem("q_done")
        k_done = sem("k_done")
        v_done = sem("v_done")
        q_ready = sem("q_ready")
        k_ready = sem("k_ready")
        s_done = sem("s_done")
        masked = sem("masked")
        max_ready = sem("max_ready")
        p_ready = sem("p_ready")
        t_done = sem("t_done")
        ta_ready = sem("ta_ready")
        td_ready = sem("td_ready")
        o_done = sem("o_done")
        o_ready = sem("o_ready")
        y_done = sem("y_done")
        r_ready = sem("r_ready")
        y_added = sem("y_added")

        stage_in = sem("stage_in")
        stage_idx = sem("stage_idx")
        scattered = sem("scattered")
        e_in = [sem(f"e_in{u}") for u in range(2)]
        et_done = sem("et_done")
        eta_ready = sem("eta_ready")
        etd_ready = sem("etd_ready")
        eu_done = sem("eu_done")
        eg_exp = sem("eg_exp")
        eh_step = sem("eh_step")
        eh_ready = sem("eh_ready")
        eht_done = sem("eht_done")
        eht_ready = sem("eht_ready")
        ed_done = sem("ed_done")
        eo_a = sem("eo_a")
        eo_d = sem("eo_d")
        eo_stored = sem("eo_stored")
        g_idx = sem("g_idx")
        gathered = [sem(f"gathered{u}") for u in range(2)]
        mix_step = sem("mix_step")
        routed_ready = sem("routed_ready")
        fin_ready = sem("fin_ready")
        out_stored = sem("out_stored")

        pro = ExitStack()

        def psb(name, shape, dt=F32):
            return pro.enter_context(nc.sbuf_tensor(name, shape, dt))

        stats = psb("stats", [P, NT, 6])
        mean = psb("mean", [P, NT])
        var = psb("var", [P, NT])
        tmp_a = psb("tmp_a", [P, NT])
        tmp_b = psb("tmp_b", [P, NT])
        std = psb("std", [P, NT])
        xn = psb("xn", [P, G4, C])
        xnt = psb("xnt", [P, KC, G4 * P])
        w_gs = psb("w_gs", [P, KC, E + 2 * HS])
        w_sd = psb("w_sd", [2 * HS, C])
        z = psb("z", [P, G4, E])
        v8 = psb("v8", [P, G4, 8])
        i8 = psb("i8", [P, G4, 8], U32)
        sg = psb("sg", [P, G4, HS])
        sh = psb("sh", [P, G4, HS])
        hsT = psb("hsT", [2 * HS, 2 * P])
        v8all = psb("v8all", [P, NT, 8])
        i8all = psb("i8all", [P, NT, 8])
        zeros = psb("zeros", [P, 4 * C])
        bvT = psb("bvT", [P, H])
        iota_e = psb("iota_e", [P, E])
        slot0 = psb("slot0", [P, E])
        tri = psb("tri", [P, P], BF16)
        ones = psb("ones", [P, P], BF16)
        eq = psb("eq", [P, NT, E])
        bvB = eq[:].rearrange("p t e -> p (t e)").rearrange("p (h m) -> p h m", h=H)
        cnt = psb("cnt", [P, NT, E])
        tot_a = psb("tot_a", [P, NT, E])
        tot_b = psb("tot_b", [P, NT, E])
        maskb = psb("maskb", [P, NT, E], BF16)
        slotf = psb("slotf", [P, NT, TOPK])
        wexp = psb("wexp", [P, NT, TOPK])
        wsum = psb("wsum", [P, NT])
        pro.close()

        stage_x = sb("stage_x", [P, 2, C])
        stage_i = sb("stage_i", [P, 2, TOPK], U32)
        stage_w = sb("stage_w", [P, 2, TOPK])
        got = sb("got", [P, 2, TOPK, C])
        part = sb("part", [P, 2, C])
        mix = sb("mix", [P, 2, C])
        ex = sb("ex", [P, 2, EG, C])
        exT = sb("exT", [P, 2, EG, KC, P])
        eup = sb("eup", [P, 2, EG, KC, 2 * HE])
        edn = sb("edn", [P, 2, C])
        eg = sb("eg", [P, 2, EG, HE])
        eh = sb("eh", [P, 2, EG, HE])
        ehT = sb("ehT", [P, 2, P])
        eo = sb("eo", [P, 2, EG, C])

        W_IN = 16 * 11

        W_IN = 16 * 12
        block = ctx.enter_context(nc.Block())

        @block.sync
        def _(sp):
            sp.dma_start(resid[:, 0:NT // 2, :], x_v[:, 0:NT // 2, :]).then_inc(x_in, 16)
            sp.dma_start(resid[:, NT // 2:, :], x_v[:, NT // 2:, :]).then_inc(x_in, 16)
            sp.dma_start(w_gs[:, :, 0:E], w_gate.rearrange("(k p) n -> p k n", p=P)).then_inc(w_in, 16)
            sp.dma_start(w_gs[:, :, E:], w_sup.rearrange("(k p) n -> p k n", p=P)).then_inc(w_in, 16)
            for n in range(2):
                sp.dma_start(w_sd[n * HS:(n + 1) * HS, :], w_sdown).then_inc(w_in, 16)
            for k in range(KC):
                sp.dma_start(wq[:, k, :], Wq[k * P:(k + 1) * P, :]).then_inc(w_in, 16)
            for g in range(2):
                sp.dma_start(wo[:, g * 8:g * 8 + 8, :], Wo.rearrange("(h d) c -> d h c", d=D)[:, g * 8:g * 8 + 8, :]).then_inc(w_in, 16)
            sp.dma_start(bqs[:], bq.rearrange("(m d) -> d m", d=D)).then_inc(w_in, 16)
            sp.dma_start(bkT[:], bk.rearrange("(m d) -> d m", d=D)).then_inc(w_in, 16)
            sp.dma_start(bvT[:], bv.rearrange("(m d) -> d m", d=D)).then_inc(w_in, 16)
            sp.dma_start(cvec[:], bo.partition_broadcast(P)).then_inc(w_in, 16)
            sp.wait_ge(const_ready, 1)
            zv = disp_d.rearrange("(n p r) c -> n p (r c)", p=P, r=4)
            for n in range(SLOTS // (4 * P)):
                sp.dma_start(zv[n], zeros[:]).then_inc(zero_stored, 16)
            sp.dma_start(eout_d[SLOTS:SLOTS + P, :], zeros[:, 0:C]).then_inc(zero_stored, 16)
            with sp.Fori(0, NG) as g:
                sp.wait_ge(xn_ready, G4 * g + G4)
                sp.dma_start(xn_d.rearrange("(t p) c -> p t c", p=P)[:, bass.ds(g * G4, G4), :], xn[:]).then_inc(xn_stored, 16)
                sp.wait_ge(xt_ready, KC * g + KC)
                sp.dma_start(xnT_d[:, :, bass.ds(g * (G4 * P), G4 * P)], xnt[:]).then_inc(xt_stored, 16)
            sp.wait_ge(xt_stored, 16 * NG)

            def head_loads(b):
                sp.wait_ge(v_done, 2 * H * b)
                sp.dma_start(xT[:], xnT_d[:, :, bass.ds(b * T, T)]).then_inc(xT_in, 16)
                with sp.Fori(0, H) as h:
                    sp.wait_ge(v_done, 2 * (H * b + h))
                    for dst, src in ((wkh, Wk), (wvh, Wv)):
                        sp.dma_start(dst[:], src.rearrange("(k p) n -> p k n", p=P)[:, :, bass.ds(h * D, D)]).then_inc(wkv_in, 16)

            head_loads(0)
            sp.wait_ge(scattered, 16 * TOPK * NT)
            with sp.Fori(0, E // EG // 2) as g:
                for u in range(2):
                    sp.wait_ge(ed_done, 2 * g)
                    sp.dma_start(ex[:, u, :, :], disp_d.rearrange("(g e p) c -> p g e c", e=EG, p=P)[:, bass.ds(2 * g + u, 1), :, :].rearrange("p a e c -> p (a e) c")).then_inc(e_in[u], 16)
                    for e in range(EG):
                        sp.dma_start(eup[:, u, e, :, :], w_up.rearrange("e (k p) n -> p e k n", p=P)[:, bass.ds((2 * g + u) * EG + e, 1), :, :].rearrange("p a k n -> p (a k) n")).then_inc(e_in[u], 16)
                    sp.dma_start(edn[:, u, :], w_down.rearrange("(g e) h c -> (e h) g c", e=EG)[:, bass.ds(2 * g + u, 1), :].rearrange("p a c -> p (a c)")).then_inc(e_in[u], 16)
            with sp.Fori(1, B) as b:
                head_loads(b)

        @block.gpsimd
        def _(pool):
            pool.memset(zeros[:], 0.0).then_inc(const_ready, 1)
            pool.memset(ident[:], 0.0).then_inc(fill_ready, 1)
            pool.memset(causal[:], 0.0).then_inc(fill_ready, 1)
            pool.memset(tri[:], 1.0).then_inc(fill_ready, 1)
            pool.memset(ones[:], 1.0).then_inc(fill_ready, 1)
            pool.iota(iota_e[:], pattern=[[1, E]], base=0, channel_multiplier=0, allow_small_or_imprecise_dtypes=True).then_inc(fill_ready, 1)
            pool.iota(slot0[:], pattern=[[CAP, E]], base=-1, channel_multiplier=0, allow_small_or_imprecise_dtypes=True).then_inc(fill_ready, 1)
            pool.wait_ge(fill_ready, 6)
            pool.affine_select(out=ident[:], in_=ident[:], compare_op=ALU.not_equal, fill=1.0, base=0,
                               pattern=[[-1, P]], channel_multiplier=1).then_inc(const_ready, 1)
            pool.affine_select(out=causal[:], in_=causal[:], compare_op=ALU.is_ge, fill=MASKED, base=0,
                               pattern=[[-1, P]], channel_multiplier=1).then_inc(const_ready, 1)
            pool.affine_select(out=tri[:], in_=tri[:], compare_op=ALU.is_ge, fill=0.0, base=0,
                               pattern=[[1, P]], channel_multiplier=-1).then_inc(const_ready, 1)

            pool.wait_ge(route_ready, 2)
            pool.wait_ge(xn_stored, 16 * NG)
            pool.wait_ge(zero_stored, 16 * (SLOTS // (4 * P) + 1))
            xn_t = xn_d.rearrange("(t p) c -> p t c", p=P)
            with pool.Fori(0, NT // 2) as tt:
                pool.wait_ge(scattered, 16 * TOPK * 2 * tt)
                pool.wait_ge(held, 2 * tt)
                pool.tensor_tensor(hold_p[:, 0:1], ident[:, 0:1], ident[:, 1:2], ALU.mult).then_inc(held, 1)
                for u in range(2):
                    pool.dma_start(stage_x[:, u, :], xn_t[:, bass.ds(2 * tt + u, 1), :].rearrange("p a c -> p (a c)")).then_inc(stage_in, 16)
                    pool.tensor_copy(stage_i[:, u, :], slot_idx[:, bass.ds(2 * tt + u, 1), :].rearrange("p a k -> p (a k)")).then_inc(stage_idx, 1)
                pool.wait_ge(stage_in, 32 * tt + 32)
                pool.wait_ge(stage_idx, 2 * tt + 2)
                pool.wait_ge(held, 2 * tt + 1)
                pool.tensor_tensor(hold_p[:, 0:1], ident[:, 0:1], ident[:, 1:2], ALU.mult).then_inc(held, 1)
                for u in range(2):
                    for k in range(TOPK):
                        pool.indirect_dma_start(
                            out=disp_d, out_offset=bass.IndirectOffsetOnAxis(ap=stage_i[:, u, k:k + 1], axis=0),
                            in_=stage_x[:, u, :], in_offset=None, bounds_check=SLOTS - 1, oob_is_err=False).then_inc(scattered, 16)

            pool.wait_ge(cvec_ready, 1)
            pool.wait_ge(eo_stored, 16 * E // EG)
            per = 2 * TOPK + 1
            with pool.Fori(0, NT // 2) as tt:
                for u in range(2):
                    pool.tensor_copy(stage_i[:, u, :], slot_idx[:, bass.ds(2 * tt + u, 1), :].rearrange("p a k -> p (a k)")).then_inc(g_idx, 1)
                    pool.tensor_copy(stage_w[:, u, :], gate_w[:, bass.ds(2 * tt + u, 1), :].rearrange("p a k -> p (a k)")).then_inc(g_idx, 1)
                pool.wait_ge(g_idx, 4 * tt + 4)
                pool.wait_ge(routed_ready, 2 * tt)
                pool.wait_ge(held, NT + tt)
                pool.tensor_tensor(hold_p[:, 0:1], ident[:, 0:1], ident[:, 1:2], ALU.mult).then_inc(held, 1)
                for u in range(2):
                    for k in range(TOPK):
                        pool.indirect_dma_start(
                            out=got[:, u, k, :], out_offset=None, in_=eout_d,
                            in_offset=bass.IndirectOffsetOnAxis(ap=stage_i[:, u, k:k + 1], axis=0),
                            bounds_check=SLOTS + P - 1, oob_is_err=False).then_inc(gathered[u], 16)
                for u in range(2):
                    pool.wait_ge(gathered[u], 16 * TOPK * (tt + 1))
                    step = 2 * TOPK * (2 * tt + u)
                    for k in range(TOPK):
                        pool.tensor_tensor(part[:, k % 2, :], got[:, u, k, :], stage_w[:, u, k:k + 1].to_broadcast([P, C]), ALU.mult).then_inc(mix_step, 1)
                        pool.wait_ge(mix_step, step + 2 * k + 1)
                        src = cvec[:] if k == 0 else mix[:, u, :]
                        pool.tensor_tensor(mix[:, u, :], part[:, k % 2, :], src, ALU.add).then_inc(mix_step, 1)
                        pool.wait_ge(mix_step, step + 2 * k + 2)
                    pool.tensor_copy(routed[:, bass.ds(2 * tt + u, 1), :].rearrange("p a c -> p (a c)"), mix[:, u, :]).then_inc(routed_ready, 1)
            for b in range(B):
                pool.wait_ge(fin_ready, b + 1)
                pool.dma_start(out_v[:, b * TB:(b + 1) * TB, :], resid[:, b * TB:(b + 1) * TB, :]).then_inc(out_stored, 16)
            pool.wait_ge(out_stored, 16 * B)

        @block.tensor
        def _(pe):
            pe.wait_ge(const_ready, 4)
            pe.wait_ge(w_in, W_IN)
            pe.wait_ge(bias_ready, 1)
            for h in range(H):
                mm = pe.matmul(ps_y[:, 0:C], bvB[:, h, :], wo[:, h, :], start=(h == 0), stop=(h == H - 1))
            mm.then_inc(cvec_done, 1)

            xt_ps = [ps_s[:, 0, 0:512], ps_s[:, 0, 512:1024]]
            g_ps = [ps_s[:, 1, 0:512], ps_s[:, 1, 512:1024]]
            d_ps = [ps_t[:, 1, :], ps_o[:]]
            NGS = E + 2 * HS
            with pe.Fori(0, NG) as g:
                for t in range(G4):
                    pe.wait_ge(xn_ready, G4 * g + t + 1)
                    for k in range(KC):
                        mm = pe.transpose(xt_ps[k][:, t * P:(t + 1) * P], xn[:, t, k * P:(k + 1) * P], ident[:])
                mm.then_inc(xt_done, 1)
                pe.wait_ge(xt_ready, KC * g + KC)
                pe.wait_ge(hs_ready, g)
                for t in range(G4):
                    for k in range(KC):
                        mm = pe.matmul(g_ps[t // 2][:, (t % 2) * NGS:(t % 2 + 1) * NGS], xnt[:, k, t * P:(t + 1) * P],
                                       w_gs[:, k, :], start=(k == 0), stop=(k == KC - 1))
                mm.then_inc(g_done, 1)
                pe.wait_ge(hs_ready, g + 1)
                for n in range(2):
                    mm = pe.transpose(ps_t[:, 0, n * P:(n + 1) * P], sh[:, 2 * n:2 * n + 2, :].rearrange("p t h -> p (t h)"), ident[:])
                mm.then_inc(ht_done, 1)
                pe.wait_ge(ht_ready, g + 1)
                pe.wait_ge(d_added, 2 * g)
                for t in range(G4):
                    half = slice((t % 2) * HS, (t % 2 + 1) * HS)
                    mm = pe.matmul(d_ps[t % 2][:, (t // 2) * C:(t // 2 + 1) * C], hsT[half, (t // 2) * P:(t // 2 + 1) * P],
                                   w_sd[half, :], start=True, stop=True)
                mm.then_inc(d_done, 1)
            pe.wait_ge(mask_ready, 1)
            pe.wait_ge(d_added, 2 * NG)
            pe.wait_ge(cvec_ready, 1)
            flat = maskb[:].rearrange("p t e -> p (t e)")
            banks = [ps_s[:, 0, 0:512], ps_s[:, 0, 512:1024], ps_s[:, 1, 0:512], ps_s[:, 1, 512:1024],
                     ps_t[:, 0, :], ps_t[:, 1, :], ps_o[:], ps_y[:]]
            for n in range(4):
                mm = pe.matmul(banks[n], tri[:], flat[:, n * 512:(n + 1) * 512], start=True, stop=True)
            for n in range(4):
                mm = pe.matmul(banks[4 + n], ones[:], flat[:, n * 512:(n + 1) * 512], start=True, stop=True)
            mm.then_inc(count_done, 1)

            def project_q(i, h, read):
                pe.wait_ge(p_ready, read)
                for m in range(H):
                    for k in range(KC):
                        mm = pe.matmul(ps_s[:, 0, m * TPH:(m + 1) * TPH], wq[:, k, m * D:(m + 1) * D],
                                       xT[:, k, bass.ds(h * TPH, TPH)], start=(k == 0), stop=(k == KC - 1))
                mm.then_inc(q_done, 1)

            def project_k(i):
                pe.wait_ge(wkv_in, 32 * i + 32)
                pe.wait_ge(p_ready, TB * i)
                for n in range(T // 512):
                    for k in range(KC):
                        mm = pe.matmul(ps_s[:, 1, n * 512:(n + 1) * 512], wkh[:, k, :],
                                       xT[:, k, n * 512:(n + 1) * 512], start=(k == 0), stop=(k == KC - 1))
                mm.then_inc(k_done, 1)

            def project_v(i):
                for n in range(2):
                    pe.wait_ge((ta_ready, td_ready)[n], 7 * i)
                    for r in range(4):
                        for k in range(KC):
                            tok = (4 * n + r) * P
                            mm = pe.matmul(ps_t[:, n, r * D:(r + 1) * D], xT[:, k, tok:tok + P], wvh[:, k, :],
                                           start=(k == 0), stop=(k == KC - 1))
                    mm.then_inc(v_done, 1)

            def scores(i, j):
                if j == 0:
                    pe.wait_ge(q_ready, i + 1)
                elif j == 1:
                    pe.wait_ge(k_ready, i + 1)
                else:
                    pe.wait_ge(p_ready, TB * i + j - 1)
                if j == 0:
                    pe.wait_ge(k_ready, i + 1)
                w = (j + 1) * P
                for lo in range(0, w, 512):
                    hi = min(w, lo + 512)
                    mm = pe.matmul(ps_s[:, j % 2, lo:hi], qT[:, j * P:(j + 1) * P], kT[:, lo:hi], start=True, stop=True)
                mm.then_inc(s_done, 1)

            chunks = [(j, c) for j in range(TB) for c in range(1 if j < 4 else 2)]

            def transposes(i, j):
                pe.wait_ge(p_ready, TB * i + j + 1)
                for n, (jj, c) in enumerate(chunks):
                    if jj != j:
                        continue
                    pe.wait_ge((ta_ready, td_ready)[n % 2], 7 * i + n // 2 + 1)
                    for r in range(4 * c, min(4 * c + 4, j + 1)):
                        mm = pe.transpose(ps_t[:, n % 2, (r - 4 * c) * P:(r - 4 * c + 1) * P],
                                          prob[:, j % 2, r * P:(r + 1) * P], ident[:])
                    mm.then_inc(t_done, 1)

            def pv(i, j):
                last = max(n for n, (jj, _) in enumerate(chunks) if jj == j)
                pe.wait_ge(ta_ready, 7 * i + 1 + (last // 2 + 1))
                pe.wait_ge(td_ready, 7 * i + 1 + (last + 1) // 2)
                pe.wait_ge(o_ready, TB * i + j)
                for r in range(j + 1):
                    mm = pe.matmul(ps_o[:, 0:P], vh[:, r, :], probT[:, j % 2, r * P:(r + 1) * P],
                                   start=(r == 0), stop=(r == j))
                mm.then_inc(o_done, 1)

            def project_y(i, h, j):
                pe.wait_ge(o_ready, TB * i + j + 1)
                pe.wait_ge(y_added, TB * i + j)
                pe.matmul(ps_y[:, 0:C], oT[:, j % 2, :], wo[:, bass.ds(h, 1), :].rearrange("p a c -> p (a c)"),
                          start=True, stop=True).then_inc(y_done, 1)

            def head(i, h, more):
                scores(i, 0)
                scores(i, 1)
                for j in range(TB):
                    transposes(i, j)
                    if j < TB - 2:
                        scores(i, j + 2)
                    elif more and j == TB - 2:
                        project_q(i + 1, h + 1, TB * i + TB - 1)
                    elif more:
                        project_k(i + 1)
                    pv(i, j)
                    if j:
                        project_y(i, h, j - 1)
                if more:
                    project_v(i + 1)
                project_y(i, h, TB - 1)

            def batch(b):
                pe.wait_ge(xT_in, 16 * b + 16)
                project_q(b * H, 0, TB * H * b)
                project_k(b * H)
                project_v(b * H)
                with pe.Fori(0, H - 1) as h:
                    head(b * H + h, h, True)
                head(b * H + (H - 1), H - 1, False)

            pe.wait_ge(route_ready, 2)
            batch(0)

            ex_ps = [[ps_s[:, u, 0:512], ps_s[:, u, 512:1024]] for u in range(2)]
            h_ps = [ps_o, ps_y]
            out_ps = [[ps_s[:, 0, 0:C], ps_s[:, 0, 512:512 + C], ps_s[:, 1, 0:C], ps_s[:, 1, 512:512 + C]],
                      [ps_t[:, 0, 0:C], ps_t[:, 1, 0:C], ps_o[:, 0:C], ps_y[:, 0:C]]]
            pe.wait_ge(y_added, TB * H)
            pe.wait_ge(p_ready, TB * H)
            with pe.Fori(0, E // EG // 2) as g:
                for u in range(2):
                    n = 2 * g + u
                    pe.wait_ge(e_in[u], 16 * (EG + 2) * (g + 1))
                    pe.wait_ge(eo_a, 2 * g)
                    pe.wait_ge(eo_d, 2 * g)
                    for e in range(EG):
                        for k in range(KC):
                            mm = pe.transpose(ex_ps[u][e // 2][:, ((e % 2) * KC + k) * P:((e % 2) * KC + k + 1) * P],
                                              ex[:, u, e, k * P:(k + 1) * P], ident[:])
                    mm.then_inc(et_done, 1)
                for u in range(2):
                    n = 2 * g + u
                    pe.wait_ge(eta_ready, n + 1)
                    pe.wait_ge(etd_ready, n + 1)
                    for e in range(EG):
                        for k in range(KC):
                            mm = pe.matmul(ps_t[:, u, e * 2 * HE:(e + 1) * 2 * HE], exT[:, u, e, k, :], eup[:, u, e, k, :],
                                           start=(k == 0), stop=(k == KC - 1))
                    mm.then_inc(eu_done, 1)
                for u in range(2):
                    n = 2 * g + u
                    pe.wait_ge(eh_ready, n + 1)
                    pe.transpose(h_ps[u][:, 0:P], eh[:, u, :, :].rearrange("p e h -> p (e h)"), ident[:]).then_inc(eht_done, 1)
                for u in range(2):
                    n = 2 * g + u
                    pe.wait_ge(eht_ready, 2 * g + 2)
                    for e in range(EG):
                        mm = pe.matmul(out_ps[u][e], ehT[e * HE:(e + 1) * HE, u, :],
                                       edn[e * HE:(e + 1) * HE, u, :], start=True, stop=True)
                    mm.then_inc(ed_done, 1)
            pe.wait_ge(eo_a, E // EG)
            pe.wait_ge(eo_d, E // EG)
            with pe.Fori(1, B) as b:
                batch(b)

        @block.scalar
        def _(act):
            act.wait_ge(stats_ready, 1)
            nc.scalar.activation(std[:], var[:], ACT.Sqrt).then_inc(std_ready, 1)

            with act.Fori(0, NG) as g:
                act.wait_ge(xt_done, g + 1)
                act.wait_ge(xt_stored, 16 * g)
                for k in range(KC):
                    nc.scalar.copy(xnt[:, k, :], ps_s[:, 0, k * 512:(k + 1) * 512]).then_inc(xt_ready, 1)
                act.wait_ge(z_step, 2 * g + 2)
                for n in range(2):
                    src = ps_s[:, 1, n * 512:n * 512 + 2 * (E + 2 * HS)].rearrange("p (t n) -> p t n", t=2)[:, :, E + HS:]
                    nc.scalar.activation(sg[:, 2 * n:2 * n + 2, :], src, ACT.Exp, scale=-1.0).then_inc(g_exp, 1)
                act.wait_ge(ht_done, g + 1)
                nc.scalar.copy(hsT[:], ps_t[:, 0, 0:2 * P]).then_inc(ht_ready, 1)
            act.wait_ge(z_read, 2 * NG)
            nc.scalar.activation(wexp[:], v8all[:, :, 0:TOPK], ACT.Exp, scale=-1.0).then_inc(logit_exp, 1)

            chunks = [(j, c) for j in range(TB) for c in range(1 if j < 4 else 2)]

            def softmax_exp(i, j):
                act.wait_ge(max_ready, TB * i + j + 1)
                w = (j + 1) * P
                nc.scalar.activation(prob[:, j % 2, 0:w], ps_s[:, j % 2, 0:w], ACT.Exp, bias=nmax[:, j:j + 1],
                                     accum_out=rsum[:, j:j + 1]).then_inc(p_ready, 1)

            def copy_transposed(i, j):
                for n, (jj, c) in enumerate(chunks):
                    if jj == j and n % 2 == 0:
                        act.wait_ge(t_done, 12 * i + n + 1)
                        w = min(4, j + 1 - 4 * c) * P
                        nc.scalar.copy(probT[:, j % 2, 4 * c * P:4 * c * P + w], ps_t[:, 0, 0:w]).then_inc(ta_ready, 1)

            def copy_k(i, h):
                act.wait_ge(k_done, i + 1)
                nc.scalar.activation(kT[:], ps_s[:, 1, :], ACT.Identity, bias=bkT[:, bass.ds(h, 1)]).then_inc(k_ready, 1)

            def copy_v(i):
                act.wait_ge(v_done, 2 * i + 1)
                nc.scalar.copy(vh[:, 0:4, :].rearrange("p r d -> p (r d)"), ps_t[:, 0, :]).then_inc(ta_ready, 1)

            def head(i, h, more):
                softmax_exp(i, 0)
                softmax_exp(i, 1)
                for j in range(TB):
                    copy_transposed(i, j)
                    if j < TB - 2:
                        softmax_exp(i, j + 2)
                    elif more and j == TB - 1:
                        copy_k(i + 1, h + 1)
                    act.wait_ge(o_done, TB * i + j + 1)
                    nc.scalar.copy(oT[:, j % 2, :], ps_o[:, 0:P]).then_inc(o_ready, 1)
                if more:
                    copy_v(i + 1)

            def batch(b):
                copy_k(b * H, 0)
                copy_v(b * H)
                with act.Fori(0, H - 1) as h:
                    head(b * H + h, h, True)
                head(b * H + (H - 1), H - 1, False)

            act.wait_ge(bias_ready, 1)
            batch(0)

            with act.Fori(0, E // EG // 2) as g:
                for u in range(2):
                    n = 2 * g + u
                    act.wait_ge(et_done, n + 1)
                    nc.scalar.copy(exT[:, u, 0:2, :, :].rearrange("p e k s -> p (e k s)"), ps_s[:, u, 0:512]).then_inc(eta_ready, 1)
                for u in range(2):
                    n = 2 * g + u
                    act.wait_ge(eu_done, n + 1)
                    src = ps_t[:, u, 0:EG * 2 * HE].rearrange("p (e n) -> p e n", e=EG)[:, :, 0:HE]
                    nc.scalar.activation(eg[:, u, :, :], src, ACT.Exp, scale=-1.0).then_inc(eg_exp, 1)
                for u in range(2):
                    n = 2 * g + u
                    act.wait_ge(eht_done, n + 1)
                    nc.scalar.copy(ehT[:, u, :], (ps_o, ps_y)[u][:, 0:P]).then_inc(eht_ready, 1)
                for u in range(2):
                    n = 2 * g + u
                    act.wait_ge(ed_done, n + 1)
                    act.wait_ge(eo_stored, 32 * g)
                    src = ps_t[:, :, 0:C] if u else ps_s[:, 0, :].rearrange("p (e c) -> p e c", e=2)[:, :, 0:C]
                    nc.scalar.copy(eo[:, u, 0:2, :], src).then_inc(eo_a, 1)
                for u in range(2):
                    n = 2 * g + u
                    act.wait_ge(eo_a, n + 1)
                    act.wait_ge(eo_d, n + 1)
                    dst = eout_d[0:SLOTS, :].rearrange("(g e p) c -> p g e c", e=EG, p=P)
                    act.dma_start(dst[:, bass.ds(n, 1), :, :].rearrange("p a e c -> p (a e) c"), eo[:, u, :, :]).then_inc(eo_stored, 16)
            with act.Fori(1, B) as b:
                batch(b)

        @block.vector
        def _(dve):
            V = nc.vector
            dve.wait_ge(x_in, 32)
            with dve.Fori(0, NT) as t:
                V.bn_stats(stats[:, bass.ds(t, 1), :].rearrange("p a s -> p (a s)"),
                           resid[:, bass.ds(t, 1), :].rearrange("p a c -> p (a c)")).then_inc(ln_step, 1)
            steps = [NT]

            def ln(ins):
                steps[0] += 1
                ins.then_inc(ln_step, 1)
                dve.wait_ge(ln_step, steps[0])

            dve.wait_ge(ln_step, NT)
            me, se, mo, so = stats[:, :, 1], stats[:, :, 2], stats[:, :, 4], stats[:, :, 5]
            ln(V.tensor_tensor(mean[:], me, mo, ALU.add))
            ln(V.tensor_scalar(mean[:], mean[:], 0.5, None, ALU.mult))
            ln(V.tensor_tensor(tmp_a[:], me, mo, ALU.subtract))
            ln(V.tensor_tensor(tmp_a[:], tmp_a[:], tmp_a[:], ALU.mult))
            ln(V.tensor_tensor(tmp_b[:], se, so, ALU.add))
            ln(V.scalar_tensor_tensor(tmp_b[:], tmp_a[:], C / 4.0, tmp_b[:], ALU.mult, ALU.add))
            V.tensor_scalar(var[:], tmp_b[:], 1.0 / C, EPS, ALU.mult, ALU.add).then_inc(stats_ready, 1)
            dve.wait_ge(std_ready, 1)
            ln(V.reciprocal(tmp_a[:], std[:]))
            ln(V.tensor_tensor(tmp_a[:], tmp_a[:], var[:], ALU.mult))
            ln(V.tensor_tensor(tmp_a[:], tmp_a[:], std[:], ALU.add))
            ln(V.tensor_scalar(tmp_a[:], tmp_a[:], 0.5, None, ALU.mult))
            ln(V.reciprocal(std[:], tmp_a[:]))
            dve.wait_ge(w_in, W_IN)
            V.tensor_scalar(bqs[:], bqs[:], SCALE, None, ALU.mult).then_inc(ln_step, 1)
            steps[0] += 1
            V.tensor_copy(bvB, bvT[:].unsqueeze(2).to_broadcast([P, H, P])).then_inc(bias_ready, 1)
            dve.wait_ge(cvec_done, 1)
            V.tensor_tensor(cvec[:], ps_y[:, 0:C], cvec[:], ALU.add).then_inc(cvec_ready, 1)

            with dve.Fori(0, NG) as g:
                dve.wait_ge(xn_stored, 16 * g)
                for t in range(G4):
                    V.tensor_scalar(xn[:, t, :], resid[:, bass.ds(g * G4 + t, 1), :].rearrange("p a c -> p (a c)"),
                                    mean[:, bass.ds(g * G4 + t, 1)], std[:, bass.ds(g * G4 + t, 1)],
                                    ALU.subtract, ALU.mult).then_inc(xn_ready, 1)
                dve.wait_ge(g_done, g + 1)
                gs = [ps_s[:, 1, n * 512:n * 512 + 2 * (E + 2 * HS)].rearrange("p (t n) -> p t n", t=2) for n in range(2)]
                for n in range(2):
                    V.tensor_scalar(z[:, 2 * n:2 * n + 2, :], gs[n][:, :, 0:E], LOGIT_LOW, LOGIT_HIGH, ALU.max, ALU.min).then_inc(z_step, 1)
                dve.wait_ge(z_step, 2 * g + 2)
                V.memset(hold_v[:], 0.0)
                for t in range(G4):
                    V.max(v8[:, t, :], z[:, t, :]).then_inc(top_step, 1)
                dve.wait_ge(top_step, 2 * G4 * g + G4)
                V.memset(hold_v[:], 0.0)
                for t in range(G4):
                    V.max_index(i8[:, t, :], v8[:, t, :], z[:, t, :]).then_inc(top_step, 1)
                V.tensor_copy(v8all[:, bass.ds(g * G4, G4), :], v8[:]).then_inc(z_read, 1)
                dve.wait_ge(top_step, 2 * G4 * g + 2 * G4)
                V.tensor_copy(i8all[:, bass.ds(g * G4, G4), :], i8[:]).then_inc(z_read, 1)
                dve.wait_ge(g_exp, 2 * g + 2)
                V.tensor_scalar(sg[:], sg[:], 1.0, None, ALU.add).then_inc(hs_step, 1)
                dve.wait_ge(hs_step, 4 * g + 1)
                V.reciprocal(sh[:], sg[:]).then_inc(hs_step, 1)
                dve.wait_ge(hs_step, 4 * g + 2)
                for n in range(2):
                    V.tensor_tensor(sg[:, 2 * n:2 * n + 2, :], gs[n][:, :, E + HS:], sh[:, 2 * n:2 * n + 2, :], ALU.mult).then_inc(hs_step, 1)
                dve.wait_ge(hs_step, 4 * g + 4)
                for n in range(2):
                    ins = V.tensor_tensor(sh[:, 2 * n:2 * n + 2, :], gs[n][:, :, E:E + HS], sg[:, 2 * n:2 * n + 2, :], ALU.mult)
                ins.then_inc(hs_ready, 1)
                dve.wait_ge(d_done, g + 1)
                for n, src in enumerate((ps_t[:, 1, :], ps_o[:])):
                    dst = resid[:, bass.ds(g * G4, G4), :].rearrange("p (a t) c -> p t a c", t=2)[:, n, :, :]
                    V.tensor_tensor(dst, src.rearrange("p (a c) -> p a c", a=2), dst, ALU.add).then_inc(d_added, 1)

            count = [0]

            def step(ins):
                count[0] += 1
                ins.then_inc(route_step, 1)
                dve.wait_ge(route_step, count[0])

            dve.wait_ge(z_read, 2 * NG)
            dve.wait_ge(const_ready, 4)
            iota_b = iota_e[:].unsqueeze(1).to_broadcast([P, NT, E])

            def choice(k):
                return i8all[:, :, k:k + 1].to_broadcast([P, NT, E])

            for k in range(TOPK):
                dst = tot_a if k == 0 else eq
                step(V.tensor_tensor(dst[:], iota_b, choice(k), ALU.is_equal))
                if k:
                    step(V.tensor_tensor(tot_a[:], tot_a[:], eq[:], ALU.add))
            V.tensor_copy(maskb[:], tot_a[:]).then_inc(mask_ready, 1)
            dve.wait_ge(count_done, 1)
            totals = (ps_t[:, 0, :], ps_t[:, 1, :], ps_o[:], ps_y[:])
            for n in range(4):
                step(V.tensor_copy(tot_a[:, 8 * n:8 * n + 8, :].rearrange("p t e -> p (t e)"), totals[n]))
            src, dst = tot_a, tot_b
            d = 1
            while d < NT:
                step(V.tensor_copy(dst[:, 0:d, :], src[:, 0:d, :]))
                step(V.tensor_tensor(dst[:, d:, :], src[:, d:, :], src[:, 0:NT - d, :], ALU.add))
                src, dst = dst, src
                d *= 2
            for n in range(4):
                got_n = ps_s[:, n // 2, (n % 2) * 512:(n % 2 + 1) * 512].rearrange("p (t e) -> p t e", t=8)
                lo = 1 if n == 0 else 0
                if n == 0:
                    step(V.tensor_copy(cnt[:, 0:1, :], got_n[:, 0:1, :]))
                step(V.tensor_tensor(cnt[:, 8 * n + lo:8 * n + 8, :], got_n[:, lo:, :], src[:, 8 * n + lo - 1:8 * n + 7, :], ALU.add))
            step(V.tensor_scalar(eq[:], cnt[:], float(CAP), 4.0 * SLOTS, ALU.is_gt, ALU.mult))
            step(V.tensor_tensor(cnt[:], cnt[:], slot0[:].unsqueeze(1).to_broadcast([P, NT, E]), ALU.add))
            step(V.tensor_tensor(cnt[:], cnt[:], eq[:], ALU.add))
            step(V.tensor_scalar(cnt[:], cnt[:], float(SLOTS), None, ALU.min))
            for k in range(TOPK):
                step(V.tensor_tensor(eq[:], iota_b, choice(k), ALU.is_equal))
                step(V.tensor_tensor(eq[:], eq[:], cnt[:], ALU.mult))
                step(V.tensor_reduce(slotf[:, :, k:k + 1], eq[:], AX.X, ALU.add))
            V.tensor_copy(slot_idx[:], slotf[:]).then_inc(route_ready, 1)
            dve.wait_ge(logit_exp, 1)
            step(V.tensor_scalar(wexp[:], wexp[:], 1.0, None, ALU.add))
            step(V.reciprocal(slotf[:], wexp[:]))
            step(V.tensor_reduce(wsum[:], slotf[:], AX.X, ALU.add))
            step(V.reciprocal(wsum[:], wsum[:]))
            V.tensor_tensor(gate_w[:], slotf[:], wsum[:].unsqueeze(2).to_broadcast([P, NT, TOPK]), ALU.mult).then_inc(route_ready, 1)

            chunks = [(j, c) for j in range(TB) for c in range(1 if j < 4 else 2)]

            def copy_q(i):
                dve.wait_ge(q_done, i + 1)
                V.scalar_tensor_tensor(
                    out=qT[:].rearrange("p (t m) -> p m t", m=H), in0=ps_s[:, 0, :].rearrange("p (m t) -> p m t", m=H),
                    scalar=SCALE, in1=bqs[:].unsqueeze(2).to_broadcast([P, H, TPH]), op0=ALU.mult, op1=ALU.add).then_inc(q_ready, 1)

            def copy_v(i):
                dve.wait_ge(v_done, 2 * i + 2)
                V.tensor_copy(vh[:, 4:8, :].rearrange("p r d -> p (r d)"), ps_t[:, 1, :]).then_inc(td_ready, 1)

            def block_max(i, j):
                dve.wait_ge(s_done, TB * i + j + 1)
                diag = ps_s[:, j % 2, j * P:(j + 1) * P]
                V.tensor_tensor(diag, diag, causal[:], ALU.add).then_inc(masked, 1)
                dve.wait_ge(masked, TB * i + j + 1)
                V.tensor_reduce(nmax[:, j:j + 1], ps_s[:, j % 2, 0:(j + 1) * P], AX.X, ALU.max, negate=True).then_inc(max_ready, 1)

            def copy_transposed(i, j):
                for n, (jj, c) in enumerate(chunks):
                    if jj == j and n % 2 == 1:
                        dve.wait_ge(t_done, 12 * i + n + 1)
                        w = min(4, j + 1 - 4 * c) * P
                        V.tensor_copy(probT[:, j % 2, 4 * c * P:4 * c * P + w], ps_t[:, 1, 0:w]).then_inc(td_ready, 1)

            def add_y(i, b, j):
                dve.wait_ge(p_ready, TB * i + j + 1)
                V.reciprocal(rinv[:, j:j + 1], rsum[:, j:j + 1]).then_inc(r_ready, 1)
                dve.wait_ge(y_done, TB * i + j + 1)
                dve.wait_ge(r_ready, TB * i + j + 1)
                row = resid[:, bass.ds(b * TB + j, 1), :].rearrange("p a c -> p (a c)")
                V.scalar_tensor_tensor(out=row, in0=ps_y[:, 0:C], scalar=rinv[:, j:j + 1], in1=row,
                                       op0=ALU.mult, op1=ALU.add).then_inc(y_added, 1)

            def head(i, b, more):
                block_max(i, 0)
                block_max(i, 1)
                for j in range(TB):
                    copy_transposed(i, j)
                    if j < TB - 2:
                        block_max(i, j + 2)
                    elif more and j == TB - 2:
                        copy_q(i + 1)
                    if j:
                        add_y(i, b, j - 1)
                if more:
                    copy_v(i + 1)
                add_y(i, b, TB - 1)

            def batch(b):
                copy_q(b * H)
                copy_v(b * H)
                with dve.Fori(0, H - 1) as h:
                    head(b * H + h, b, True)
                head(b * H + (H - 1), b, False)

            def finish(b):
                dve.wait_ge(routed_ready, TB * b + TB)
                dve.wait_ge(y_added, TB * H * (b + 1))
                rows = resid[:, bass.ds(b * TB, TB), :].rearrange("p t c -> p (t c)")
                V.tensor_tensor(rows, rows, routed[:, bass.ds(b * TB, TB), :].rearrange("p t c -> p (t c)"), ALU.add).then_inc(fin_ready, 1)

            dve.wait_ge(ln_step, steps[0])
            batch(0)

            with dve.Fori(0, E // EG // 2) as g:
                for u in range(2):
                    n = 2 * g + u
                    dve.wait_ge(et_done, n + 1)
                    V.tensor_copy(exT[:, u, 2:4, :, :].rearrange("p e k s -> p (e k s)"), ps_s[:, u, 512:1024]).then_inc(etd_ready, 1)
                for u in range(2):
                    n = 2 * g + u
                    up = ps_t[:, u, 0:EG * 2 * HE].rearrange("p (e n) -> p e n", e=EG)
                    dve.wait_ge(eg_exp, n + 1)
                    V.tensor_scalar(eg[:, u], eg[:, u], 1.0, None, ALU.add).then_inc(eh_step, 1)
                    dve.wait_ge(eh_step, 3 * n + 1)
                    V.reciprocal(eh[:, u], eg[:, u]).then_inc(eh_step, 1)
                    dve.wait_ge(eh_step, 3 * n + 2)
                    V.tensor_tensor(eg[:, u], up[:, :, 0:HE], eh[:, u], ALU.mult).then_inc(eh_step, 1)
                    dve.wait_ge(eh_step, 3 * n + 3)
                    V.tensor_tensor(eh[:, u], up[:, :, HE:], eg[:, u], ALU.mult).then_inc(eh_ready, 1)
                for u in range(2):
                    n = 2 * g + u
                    dve.wait_ge(ed_done, n + 1)
                    dve.wait_ge(eo_stored, 32 * g)
                    if u:
                        V.tensor_copy(eo[:, u, 2, :], ps_o[:, 0:C])
                        V.tensor_copy(eo[:, u, 3, :], ps_y[:, 0:C]).then_inc(eo_d, 1)
                    else:
                        V.tensor_copy(eo[:, u, 2:4, :], ps_s[:, 1, :].rearrange("p (e c) -> p e c", e=2)[:, :, 0:C]).then_inc(eo_d, 1)
            with dve.Fori(1, B) as b:
                batch(b)
                finish(b - 1)
            finish(B - 1)


_INS = ["L0_attn_x", "L0_attn_Wq", "L0_attn_bq", "L0_attn_Wk", "L0_attn_bk", "L0_attn_Wv", "L0_attn_bv", "L0_attn_Wo",
        "L0_attn_bo", "L0_ffn_w_gate", "L0_ffn_w_shared_up", "L0_ffn_w_shared_down", "L0_ffn_w_up", "L0_ffn_w_down"]


def kernel(**inputs):
    import numpy as _np
    import concourse.bacc as _bacc
    from concourse import mybir as _mybir
    from concourse.bass_utils import run_bass_kernel_spmd as _run

    nc = _bacc.Bacc("TRN2", target_bir_lowering=False, num_devices=1)
    arrays, args = {}, []
    for name in _INS:
        a = _np.ascontiguousarray(inputs[name])
        arrays[f"in_{name}_dram"] = a
        args.append(nc.dram_tensor(f"in_{name}_dram", a.shape, _mybir.dt.from_np(a.dtype), kind="ExternalInput").ap())
    shape = inputs["L0_attn_x"].shape
    args.append(nc.dram_tensor("out_0_dram", shape, _mybir.dt.from_np(_np.dtype("float32")), kind="ExternalOutput").ap())
    causal_attention_with_moe(nc, *args)
    r = _run(nc, [arrays], core_ids=[0])
    return r.results[0]["out_0_dram"]
```

```python
from contextlib import ExitStack

import concourse.bass as bass
from concourse import mybir

F32 = mybir.dt.float32
BF16 = mybir.dt.bfloat16
F16 = mybir.dt.float16
RMAX = bass.bass_isa.ReduceOp.max
U32 = mybir.dt.uint32
ALU = mybir.AluOpType
ACT = mybir.ActivationFunctionType
AX = mybir.AxisListType

P = 128
TOPK = 6
CAP = 128
EPS = 1e-5
MASKED = -3.0e38
LOGIT_LOW, LOGIT_HIGH = -104.0, 16.7
XN_BOUND = 16.0
TOP = 15
O_SHIFT = 2.0 ** -10


def causal_attention_with_moe(nc, x, Wq, bq, Wk, bk, Wv, bv, Wo, bo, w_gate, w_sup, w_sdown, w_up, w_down, out):
    B, T, C = x.shape
    HD = Wq.shape[1]
    D = 128
    H = HD // D
    SCALE = float(D) ** -0.5
    KC = C // P
    NT = B * T // P
    TB = T // P
    TPH = T // H
    E = w_gate.shape[1]
    HE = w_down.shape[1]
    HS = w_sdown.shape[0]
    G4 = 4
    NG = NT // G4
    EG = 4
    SLOTS = E * CAP
    assert C == 256 and T == 1024 and H == 16 and E == 64 and EG * HE == P and H * D == HD

    xn_d = nc.dram_tensor("xn_rows", (NT * P, C), F32, kind="Internal").ap()
    xnT_d = nc.dram_tensor("xn_columns", (P, 2, KC, NT * P), F16, kind="Internal").ap()
    routed_d = nc.dram_tensor("routed", (P, NT, C), F32, kind="Internal").ap()
    disp_d = nc.dram_tensor("dispatched", (SLOTS, C), F32, kind="Internal").ap()
    eout_d = nc.dram_tensor("expert_out", (SLOTS + P, C), F32, kind="Internal").ap()

    x_v = x.rearrange("b (t p) c -> p (b t) c", p=P)
    out_v = out.rearrange("b (t p) c -> p (b t) c", p=P)

    with ExitStack() as ctx:
        def sb(name, shape, dt=F32):
            return ctx.enter_context(nc.sbuf_tensor(name, shape, dt))

        def sem(name):
            return ctx.enter_context(nc.semaphore(name))

        ctx.enter_context(nc.allow_non_contiguous_dma("small bias columns and weight slices"))

        resid = sb("resid", [P, NT, C])
        cvec = sb("cvec", [P, C])
        ident = sb("ident", [P, P])
        identb = sb("identb", [P, P], BF16)
        causal = sb("causal", [P, P], BF16)
        wq = sb("wq", [P, 2, KC, HD], F16)
        wk = sb("wk", [P, 2, KC, HD], F16)
        wv = sb("wv", [P, 2, KC, HD], F16)
        wo = sb("wo", [P, 2, H, C], F16)
        bqT = sb("bqT", [P, H])
        bkT = sb("bkT", [P, H])
        scales = sb("scales", [P, 4])
        logit_scale = sb("logit_scale", [P, 1])
        out_scale = sb("out_scale", [P, 1])
        slot_idx = sb("slot_idx", [P, NT, TOPK], U32)
        gate_w = sb("gate_w", [P, NT, TOPK])
        hold_v = sb("hold_v", [P, 3])
        hold_a = sb("hold_a", [P, 3])
        hold_p = sb("hold_p", [P, 2])

        stage_x = sb("stage_x", [P, 2, C])
        stage_i = sb("stage_i", [P, 2, TOPK], U32)
        stage_w = sb("stage_w", [P, 2, TOPK])
        got = sb("got", [P, 2, TOPK, C])
        part = sb("part", [P, 2, C])
        mix = sb("mix", [P, 2, C])

        ps_s = ctx.enter_context(nc.psum_tensor("ps_s", [P, 2, 2 * 512], F32))
        ps_t = ctx.enter_context(nc.psum_tensor("ps_t", [P, 2, 512], F32))
        ps_o = ctx.enter_context(nc.psum_tensor("ps_o", [P, 512], F32))
        ps_y = ctx.enter_context(nc.psum_tensor("ps_y", [P, 512], F32))

        x_in = sem("x_in")
        w_in = sem("w_in")
        const_ready = sem("const_ready")
        bias_ready = sem("bias_ready")
        fill_ready = sem("fill_ready")
        held = sem("held")
        stats_ready = sem("stats_ready")
        std_ready = sem("std_ready")
        ln_step = sem("ln_step")
        cvec_done = sem("cvec_done")
        cvec_ready = sem("cvec_ready")
        xn_ready = sem("xn_ready")
        xn_stored = sem("xn_stored")
        xn_high = sem("xn_high")
        xt_done = sem("xt_done")
        xt_ready = sem("xt_ready")
        xt_stored = sem("xt_stored")
        g_done = sem("g_done")
        g_exp = sem("g_exp")
        z_step = sem("z_step")
        top_step = sem("top_step")
        z_read = sem("z_read")
        hs_step = sem("hs_step")
        hs_ready = sem("hs_ready")
        ht_done = sem("ht_done")
        ht_ready = sem("ht_ready")
        d_done = sem("d_done")
        d_added = sem("d_added")
        route_step = sem("route_step")
        mask_ready = sem("mask_ready")
        count_done = sem("count_done")
        logit_exp = sem("logit_exp")
        route_ready = sem("route_ready")
        zero_stored = sem("zero_stored")

        xT_in = sem("xT_in")
        q_done = sem("q_done")
        k_done = sem("k_done")
        qf_ready = sem("qf_ready")
        q_ready = sem("q_ready")
        q_high = sem("q_high")
        k_high = sem("k_high")
        k_ready = sem("k_ready")
        s_done = sem("s_done")
        max_step = sem("max_step")
        max_ready = sem("max_ready")
        p_ready = sem("p_ready")
        t_done = sem("t_done")
        t_high = sem("t_high")
        t_ready = sem("t_ready")
        o_done = sem("o_done")
        o_high = sem("o_high")
        o_ready = sem("o_ready")
        y_done = sem("y_done")
        r_step = sem("r_step")
        r_ready = sem("r_ready")
        y_added = sem("y_added")
        wmax_step = sem("wmax_step")
        bounds_ready = sem("bounds_ready")
        wscale_step = sem("wscale_step")
        scale_ready = sem("scale_ready")
        whigh = sem("whigh")
        wsplit = sem("wsplit")
        xn_low = sem("xn_low")
        wload = [sem(f"wload{n}") for n in range(2)]
        wreload = [sem(f"wreload{n}") for n in range(2)]

        stage_in = sem("stage_in")
        stage_idx = sem("stage_idx")
        scattered = sem("scattered")
        ex_in = [sem(f"ex_in{u}") for u in range(2)]
        eup_in = [sem(f"eup_in{u}") for u in range(2)]
        edn_in = [sem(f"edn_in{u}") for u in range(2)]
        et_done = sem("et_done")
        eta_ready = sem("eta_ready")
        etd_ready = sem("etd_ready")
        eu_done = sem("eu_done")
        eg_exp = sem("eg_exp")
        eh_step = sem("eh_step")
        eh_ready = sem("eh_ready")
        eht_done = sem("eht_done")
        eht_ready = sem("eht_ready")
        ed_done = sem("ed_done")
        eo_a = sem("eo_a")
        eo_d = sem("eo_d")
        eo_stored = sem("eo_stored")
        g_idx = sem("g_idx")
        gathered = [sem(f"gathered{u}") for u in range(2)]
        mix_step = sem("mix_step")
        routed_ready = sem("routed_ready")
        fin_ready = sem("fin_ready")
        routed_in = sem("routed_in")
        out_stored = sem("out_stored")

        pro = ExitStack()

        def psb(name, shape, dt=F32):
            return pro.enter_context(nc.sbuf_tensor(name, shape, dt))

        stats = psb("stats", [P, NT, 6])
        mean = psb("mean", [P, NT])
        var = psb("var", [P, NT])
        tmp_a = psb("tmp_a", [P, NT])
        tmp_b = psb("tmp_b", [P, NT])
        std = psb("std", [P, NT])
        xn = psb("xn", [P, G4, C])
        xnt = psb("xnt", [P, KC, G4 * P])
        xnth = psb("xnth", [P, 2, KC, G4 * P], F16)
        work = psb("work", [P, 4 * NT * E])
        stg = [work[:, 0:2 * NT * E], work[:, 2 * NT * E:]]
        bvB = psb("bvB", [P, H, P])
        absmax = psb("absmax", [P, 4])
        biasmax = psb("biasmax", [P, 2])
        bound = psb("bound", [P, 4])
        bounds = psb("bounds", [P, 4])
        expo_u = psb("expo_u", [P, 4], U32)
        expo = psb("expo", [P, 4])
        sinv_u = psb("sinv_u", [P, 4], U32)
        scale_u = psb("scale_u", [P, 4], U32)
        w_gs = psb("w_gs", [P, KC, E + 2 * HS])
        w_sd = psb("w_sd", [2 * HS, C])
        z = psb("z", [P, G4, E])
        v8 = psb("v8", [P, G4, 8])
        i8 = psb("i8", [P, G4, 8], U32)
        sg = psb("sg", [P, G4, HS])
        sh = psb("sh", [P, G4, HS])
        hsT = psb("hsT", [2 * HS, 2 * P])
        v8all = psb("v8all", [P, NT, 8])
        i8all = psb("i8all", [P, NT, 8])
        zeros = psb("zeros", [P, 4 * C])
        bvT = psb("bvT", [P, H])
        iota_e = psb("iota_e", [P, E])
        slot0 = psb("slot0", [P, E])
        tri = psb("tri", [P, P], BF16)
        ones = psb("ones", [P, P], BF16)
        eq, cnt, tot_a, tot_b = [work[:, n * NT * E:(n + 1) * NT * E].rearrange("p (t e) -> p t e", t=NT) for n in range(4)]
        maskb = psb("maskb", [P, NT, E], BF16)
        i8b = psb("i8b", [P, NT, 8], BF16)
        iota_b16 = psb("iota_b16", [P, E], BF16)
        slotf = psb("slotf", [P, NT, TOPK])
        wexp = psb("wexp", [P, NT, TOPK])
        wsum = psb("wsum", [P, NT])
        pro.close()

        xT = sb("xT", [P, 2, KC, T], F16)
        qf = sb("qf", [P, T])
        qT = sb("qT", [P, 2, 2, T], F16)
        kT = sb("kT", [P, 2, 2, T], F16)
        vh = sb("vh", [P, 2, 2, TB * D], F16)
        nmax0 = sb("nmax0", [P, TB])
        nmax = sb("nmax", [P, TB])
        rsum = sb("rsum", [P, TB])
        rinv = sb("rinv", [P, TB])
        yscale = sb("yscale", [P, TB])
        tmp = ExitStack()
        prob = tmp.enter_context(nc.sbuf_tensor("prob", [P, 2, T], F32))
        probT = tmp.enter_context(nc.sbuf_tensor("probT", [P, 2, 2, T], F16))
        oT = tmp.enter_context(nc.sbuf_tensor("oT", [P, 2, 2, P], F16))
        oF = tmp.enter_context(nc.sbuf_tensor("oF", [P, 2, P], F32))
        tmp.close()
        ex = sb("ex", [P, 2, EG, C])
        exT = sb("exT", [P, 2, EG, KC, P])
        eup = sb("eup", [P, 2, EG, KC, 2 * HE])
        edn = sb("edn", [P, 2, C])
        eg = sb("eg", [P, 2, EG, HE])
        eh = sb("eh", [P, 2, EG, HE])
        ehT = sb("ehT", [P, 2, P])
        eo = sb("eo", [P, 2, EG, C])

        W_IN = 16 * 8
        WSTEPS = 8 + 9 + 7

        T_RING = [("T", 0, 0), ("T", 1, 0), ("T", 2, 0), ("V", 0, 0), ("T", 3, 0), ("V", 1, 0)]
        T_RING += [("T", j, c) for j in range(4, TB) for c in range(2)]
        V_RING = [n for n, (what, _, _) in enumerate(T_RING) if what == "V"]
        RING = len(T_RING)

        def ring_count(i, n, project=True):
            left_out = 0 if project else sum(what == "V" for what, _, _ in T_RING[:n])
            return RING * i + n - left_out + 3

        def bank_count(i, n, project=True):
            m = n - 2
            while not project and m >= 0 and T_RING[m][0] == "V":
                m -= 2
            return RING * i + n + 1 if m < 0 else ring_count(i, m, project)
        S_SLOT = [0, 1, 0, 0, 0, 1, 0, 1]
        block = ctx.enter_context(nc.Block())
        views = [Wq.rearrange("(k p) n -> p k n", p=P), Wk.rearrange("(k p) n -> p k n", p=P),
                 Wv.rearrange("(k p) n -> p k n", p=P), Wo.rearrange("(h d) c -> d h c", d=D)]

        @block.sync
        def _(sp):
            sp.dma_start(resid[:, 0:NT // 2, :], x_v[:, 0:NT // 2, :]).then_inc(x_in, 16)
            sp.dma_start(resid[:, NT // 2:, :], x_v[:, NT // 2:, :]).then_inc(x_in, 16)
            sp.dma_start(w_gs[:, :, 0:E], w_gate.rearrange("(k p) n -> p k n", p=P)).then_inc(w_in, 16)
            sp.dma_start(w_gs[:, :, E:], w_sup.rearrange("(k p) n -> p k n", p=P)).then_inc(w_in, 16)
            for n in range(2):
                sp.dma_start(stg[n].rearrange("p (k n) -> p k n", k=KC), views[n]).then_inc(wload[n], 16)
            for n in range(2):
                sp.dma_start(w_sd[n * HS:(n + 1) * HS, :], w_sdown).then_inc(w_in, 16)
            sp.dma_start(bqT[:], bq.rearrange("(m d) -> d m", d=D)).then_inc(w_in, 16)
            sp.dma_start(bkT[:], bk.rearrange("(m d) -> d m", d=D)).then_inc(w_in, 16)
            sp.dma_start(bvT[:], bv.rearrange("(m d) -> d m", d=D)).then_inc(w_in, 16)
            sp.dma_start(cvec[:], bo.partition_broadcast(P)).then_inc(w_in, 16)
            with sp.Fori(0, NG) as g:
                sp.wait_ge(xn_ready, G4 * g + G4)
                sp.dma_start(xn_d.rearrange("(t p) c -> p t c", p=P)[:, bass.ds(g * G4, G4), :], xn[:]).then_inc(xn_stored, 16)
                sp.wait_ge(xn_low, KC * g + KC)
                for n in range(2):
                    sp.dma_start(xnT_d[:, n, :, bass.ds(g * (G4 * P), G4 * P)], xnth[:, n, :, :]).then_inc(xt_stored, 16)
            sp.wait_ge(const_ready, 1)
            zv = disp_d.rearrange("(n p r) c -> n p (r c)", p=P, r=4)
            for n in range(SLOTS // (4 * P)):
                sp.dma_start(zv[n], zeros[:]).then_inc(zero_stored, 16)
            sp.dma_start(eout_d[SLOTS:SLOTS + P, :], zeros[:, 0:C]).then_inc(zero_stored, 16)
            sp.wait_ge(xt_stored, 32 * NG)

            def load_xT(b):
                if b:
                    sp.wait_ge(t_done, ring_count(H * b - 2, V_RING[1]))
                for n in range(2):
                    sp.dma_start(xT[:, n, :, :], xnT_d[:, n, :, b * T:(b + 1) * T]).then_inc(xT_in, 16)

            sp.wait_ge(route_ready, 2)
            load_xT(0)
            load_xT(1)
            sp.wait_ge(scattered, 16 * TOPK * NT)
            sp.wait_ge(y_added, TB * H + 1)
            rows_v = disp_d.rearrange("(g e p) c -> p g e c", e=EG, p=P)
            up_v = w_up.rearrange("e (k p) n -> p e k n", p=P)
            down_v = w_down.rearrange("(g e) h c -> (e h) g c", e=EG)

            def load_experts(g, first):
                for u in range(2):
                    if not first:
                        sp.wait_ge(et_done, 2 * g + u - 1)
                    sp.dma_start(ex[:, u, :, :], rows_v[:, bass.ds(2 * g + u, 1), :, :].rearrange("p a e c -> p (a e) c")).then_inc(ex_in[u], 16)
                for u in range(2):
                    if not first:
                        sp.wait_ge(eu_done, 2 * g + u - 1)
                    for e in range(EG):
                        sp.dma_start(eup[:, u, e, :, :], up_v[:, bass.ds((2 * g + u) * EG + e, 1), :, :].rearrange("p a k n -> p (a k) n")).then_inc(eup_in[u], 16)
                for u in range(2):
                    if not first:
                        sp.wait_ge(ed_done, 2 * g + u - 1)
                    sp.dma_start(edn[:, u, :], down_v[:, bass.ds(2 * g + u, 1), :].rearrange("p a c -> p (a c)")).then_inc(edn_in[u], 16)

            load_experts(0, True)
            with sp.Fori(1, E // EG // 2) as g:
                load_experts(g, False)
            for b in range(2, B):
                load_xT(b)

        @block.gpsimd
        def _(pool):
            pool.memset(zeros[:], 0.0).then_inc(const_ready, 1)
            pool.memset(ident[:], 0.0).then_inc(fill_ready, 1)
            pool.memset(identb[:], 0.0).then_inc(fill_ready, 1)
            pool.memset(causal[:], 0.0).then_inc(fill_ready, 1)
            pool.memset(tri[:], 1.0).then_inc(fill_ready, 1)
            pool.memset(ones[:], 1.0).then_inc(fill_ready, 1)
            pool.iota(iota_e[:], pattern=[[1, E]], base=0, channel_multiplier=0, allow_small_or_imprecise_dtypes=True).then_inc(fill_ready, 1)
            pool.iota(slot0[:], pattern=[[CAP, E]], base=-1, channel_multiplier=0, allow_small_or_imprecise_dtypes=True).then_inc(fill_ready, 1)
            pool.wait_ge(fill_ready, 7)
            pool.affine_select(out=ident[:], in_=ident[:], compare_op=ALU.not_equal, fill=1.0, base=0,
                               pattern=[[-1, P]], channel_multiplier=1).then_inc(const_ready, 1)
            pool.affine_select(out=identb[:], in_=identb[:], compare_op=ALU.not_equal, fill=1.0, base=0,
                               pattern=[[-1, P]], channel_multiplier=1).then_inc(const_ready, 1)
            pool.affine_select(out=causal[:], in_=causal[:], compare_op=ALU.is_ge, fill=MASKED, base=0,
                               pattern=[[-1, P]], channel_multiplier=1).then_inc(const_ready, 1)
            pool.affine_select(out=tri[:], in_=tri[:], compare_op=ALU.is_ge, fill=0.0, base=0,
                               pattern=[[1, P]], channel_multiplier=-1).then_inc(const_ready, 1)

            for r in range(2):
                pool.wait_ge(bounds_ready, r + 1)
                pool.partition_all_reduce(bounds[:, 2 * r:2 * r + 2], bound[:, 2 * r:2 * r + 2], P, RMAX).then_inc(scale_ready, 1)
                for n in range(2):
                    w = (wq, wk, wv, wo)[2 * r + n]
                    pool.wait_ge(whigh, 2 * r + n + 1)
                    pool.tensor_tensor(w[:, 1, :, :].rearrange("p a b -> p (a b)"), stg[n],
                                       w[:, 0, :, :].rearrange("p a b -> p (a b)"), ALU.subtract).then_inc(wsplit, 1)
                    if r == 0:
                        pool.wait_ge(wsplit, n + 1)
                        pool.dma_start(stg[n].rearrange("p (k n) -> p k n", k=(KC, H)[n]), views[2 + n]).then_inc(wreload[n], 16)

            pool.wait_ge(route_ready, 2)
            pool.wait_ge(xn_stored, 16 * NG)
            pool.wait_ge(zero_stored, 16 * (SLOTS // (4 * P) + 1))
            xn_t = xn_d.rearrange("(t p) c -> p t c", p=P)
            def dispatch(tt, first):
                if not first:
                    pool.wait_ge(scattered, 16 * TOPK * 2 * tt)
                    pool.wait_ge(held, 2 * tt)
                pool.tensor_tensor(hold_p[:, 0:1], ident[:, 0:1], ident[:, 1:2], ALU.mult).then_inc(held, 1)
                for u in range(2):
                    pool.dma_start(stage_x[:, u, :], xn_t[:, bass.ds(2 * tt + u, 1), :].rearrange("p a c -> p (a c)")).then_inc(stage_in, 16)
                    pool.tensor_copy(stage_i[:, u, :], slot_idx[:, bass.ds(2 * tt + u, 1), :].rearrange("p a k -> p (a k)")).then_inc(stage_idx, 1)
                pool.wait_ge(stage_in, 32 * tt + 32)
                pool.wait_ge(stage_idx, 2 * tt + 2)
                pool.wait_ge(held, 2 * tt + 1)
                pool.tensor_tensor(hold_p[:, 0:1], ident[:, 0:1], ident[:, 1:2], ALU.mult).then_inc(held, 1)
                for u in range(2):
                    for k in range(TOPK):
                        pool.indirect_dma_start(
                            out=disp_d, out_offset=bass.IndirectOffsetOnAxis(ap=stage_i[:, u, k:k + 1], axis=0),
                            in_=stage_x[:, u, :], in_offset=None, bounds_check=SLOTS - 1, oob_is_err=False).then_inc(scattered, 16)

            dispatch(0, True)
            with pool.Fori(1, NT // 2) as tt:
                dispatch(tt, False)

            pool.wait_ge(cvec_ready, 1)
            pool.wait_ge(eo_stored, 16 * E // EG)
            per = 2 * TOPK + 1
            def combine(tt, first):
                for u in range(2):
                    pool.tensor_copy(stage_i[:, u, :], slot_idx[:, bass.ds(2 * tt + u, 1), :].rearrange("p a k -> p (a k)")).then_inc(g_idx, 1)
                    pool.tensor_copy(stage_w[:, u, :], gate_w[:, bass.ds(2 * tt + u, 1), :].rearrange("p a k -> p (a k)")).then_inc(g_idx, 1)
                pool.wait_ge(g_idx, 4 * tt + 4)
                if not first:
                    pool.wait_ge(routed_ready, 32 * tt)
                pool.wait_ge(held, NT + tt)
                pool.tensor_tensor(hold_p[:, 0:1], ident[:, 0:1], ident[:, 1:2], ALU.mult).then_inc(held, 1)
                for u in range(2):
                    for k in range(TOPK):
                        pool.indirect_dma_start(
                            out=got[:, u, k, :], out_offset=None, in_=eout_d,
                            in_offset=bass.IndirectOffsetOnAxis(ap=stage_i[:, u, k:k + 1], axis=0),
                            bounds_check=SLOTS + P - 1, oob_is_err=False).then_inc(gathered[u], 16)
                for u in range(2):
                    pool.wait_ge(gathered[u], 16 * TOPK * (tt + 1))
                    step = 2 * TOPK * (2 * tt + u)
                    for k in range(TOPK):
                        pool.tensor_tensor(part[:, k % 2, :], got[:, u, k, :], stage_w[:, u, k:k + 1].to_broadcast([P, C]), ALU.mult).then_inc(mix_step, 1)
                        pool.wait_ge(mix_step, step + 2 * k + 1)
                        src = cvec[:] if k == 0 else mix[:, u, :]
                        pool.tensor_tensor(mix[:, u, :], part[:, k % 2, :], src, ALU.add).then_inc(mix_step, 1)
                        pool.wait_ge(mix_step, step + 2 * k + 2)
                    pool.dma_start(routed_d[:, bass.ds(2 * tt + u, 1), :].rearrange("p a c -> p (a c)"), mix[:, u, :]).then_inc(routed_ready, 16)

            combine(0, True)
            with pool.Fori(1, NT // 2) as tt:
                combine(tt, False)
            pool.wait_ge(routed_ready, 16 * NT)
            rows = got[:].rearrange("p u k c -> p (u k) c")[:, 0:TB, :]
            for b in range(B):
                if b:
                    pool.wait_ge(fin_ready, b)
                pool.dma_start(rows, routed_d[:, b * TB:(b + 1) * TB, :]).then_inc(routed_in, 16)
                tiles = resid[:, b * TB:(b + 1) * TB, :]
                if b < B - 1:
                    pool.wait_ge(routed_in, 16 * (b + 1))
                    pool.wait_ge(y_added, TB * H * (b + 1) + 1)
                    pool.tensor_tensor(tiles, tiles, rows, ALU.add).then_inc(fin_ready, 1)
                pool.wait_ge(fin_ready, b + 1)
                pool.dma_start(out_v[:, b * TB:(b + 1) * TB, :], tiles).then_inc(out_stored, 16)
            pool.wait_ge(out_stored, 16 * B)

        @block.tensor
        def _(pe):
            pe.wait_ge(const_ready, 5)
            pe.wait_ge(w_in, W_IN)
            xt_ps = [ps_s[:, 0, 0:512], ps_s[:, 0, 512:1024]]
            g_ps = [ps_s[:, 1, 0:512], ps_s[:, 1, 512:1024]]
            d_ps = [ps_t[:, 1, :], ps_o[:]]
            NGS = E + 2 * HS

            def transpose_x(g):
                for t in range(G4):
                    pe.wait_ge(xn_ready, G4 * g + t + 1)
                    for k in range(KC):
                        mm = pe.transpose(xt_ps[k][:, t * P:(t + 1) * P], xn[:, t, k * P:(k + 1) * P], ident[:])
                mm.then_inc(xt_done, 1)

            def shared_down(g, first):
                pe.wait_ge(ht_ready, g + 1)
                if not first:
                    pe.wait_ge(d_added, 2 * g)
                for t in range(G4):
                    half = slice((t % 2) * HS, (t % 2 + 1) * HS)
                    mm = pe.matmul(d_ps[t % 2][:, (t // 2) * C:(t // 2 + 1) * C], hsT[half, (t // 2) * P:(t // 2 + 1) * P],
                                   w_sd[half, :], start=True, stop=True)
                mm.then_inc(d_done, 1)

            def group(g, before, after):
                pe.wait_ge(xt_ready, KC * g + KC)
                if before:
                    pe.wait_ge(hs_ready, g)
                for t in range(G4):
                    for k in range(KC):
                        mm = pe.matmul(g_ps[t // 2][:, (t % 2) * NGS:(t % 2 + 1) * NGS], xnt[:, k, t * P:(t + 1) * P],
                                       w_gs[:, k, :], start=(k == 0), stop=(k == KC - 1))
                mm.then_inc(g_done, 1)
                if before:
                    shared_down(g - 1, before == 1)
                if after:
                    transpose_x(g + 1)
                pe.wait_ge(hs_ready, g + 1)
                for n in range(2):
                    mm = pe.transpose(ps_t[:, 0, n * P:(n + 1) * P], sh[:, 2 * n:2 * n + 2, :].rearrange("p t h -> p (t h)"), ident[:])
                mm.then_inc(ht_done, 1)

            transpose_x(0)
            group(0, 0, True)
            pe.wait_ge(bias_ready, 1)
            pe.wait_ge(wreload[1], 16)
            for h in range(H):
                mm = pe.matmul(ps_y[:, 0:C], bvB[:, h, :], stg[1][:, h * C:(h + 1) * C], start=(h == 0), stop=(h == H - 1))
            mm.then_inc(cvec_done, 1)
            group(1, 1, True)
            with pe.Fori(2, NG - 1) as g:
                group(g, 2, True)
            group(NG - 1, 2, False)
            shared_down(NG - 1, False)
            pe.wait_ge(mask_ready, 1)
            pe.wait_ge(d_added, 2 * NG)
            pe.wait_ge(cvec_ready, 1)
            flat = maskb[:].rearrange("p t e -> p (t e)")
            banks = [ps_s[:, 0, 0:512], ps_s[:, 0, 512:1024], ps_s[:, 1, 0:512], ps_s[:, 1, 512:1024],
                     ps_t[:, 0, :], ps_t[:, 1, :], ps_o[:], ps_y[:]]
            for n in range(4):
                mm = pe.matmul(banks[n], tri[:], flat[:, n * 512:(n + 1) * 512], start=True, stop=True)
            for n in range(4):
                mm = pe.matmul(banks[4 + n], ones[:], flat[:, n * 512:(n + 1) * 512], start=True, stop=True)
            mm.then_inc(count_done, 1)

            PASSES = ((0, 0), (0, 1), (1, 0))

            def project_q(i, s, h):
                for m in range(H):
                    if m % (H // 2) == 0:
                        pe.wait_ge(k_ready, 2 * i + 2 * m // H + 1)
                    for n, (a, c) in enumerate(PASSES):
                        for k in range(KC):
                            mm = pe.matmul(ps_s[:, 1, m * TPH:(m + 1) * TPH], wq[:, a, k, m * D:(m + 1) * D],
                                           xT[:, c, k, bass.ds(h * TPH, TPH)], start=(n + k == 0), stop=(n + k == 3))
                    if m % (H // 2) == H // 2 - 1:
                        mm.then_inc(q_done, 1)

            def project_k(s, h):
                for half in range(T // 512):
                    for n, (a, c) in enumerate(PASSES):
                        for k in range(KC):
                            mm = pe.matmul(ps_s[:, 1, half * 512:(half + 1) * 512], wk[:, a, k, bass.ds(h * D, D)],
                                           xT[:, c, k, half * 512:(half + 1) * 512], start=(n + k == 0), stop=(n + k == 3))
                    mm.then_inc(k_done, 1)

            def project_v(h, half, bank):
                for r in range(4):
                    tok = (4 * half + r) * P
                    for n, (a, c) in enumerate(PASSES):
                        for k in range(KC):
                            mm = pe.matmul(ps_t[:, bank, r * D:(r + 1) * D], xT[:, a, k, tok:tok + P],
                                           wv[:, c, k, bass.ds(h * D, D)], start=(n + k == 0), stop=(n + k == 3))
                mm.then_inc(t_done, 1)

            def scores(u, j):
                w = (j + 1) * P
                slot = S_SLOT[j]
                for lo in range(0, w, 512):
                    hi = min(w, lo + 512)
                    for n, (a, c) in enumerate(PASSES):
                        mm = pe.matmul(ps_s[:, slot, lo:hi], qT[:, u, a, j * P:(j + 1) * P], kT[:, u, c, lo:hi],
                                       start=(n == 0), stop=(n == 2 and hi < w))
                pe.matmul(ps_s[:, slot, j * P:w], identb[:], causal[:], start=False, stop=True).then_inc(s_done, 1)

            def transposes(i, j, project):
                pe.wait_ge(p_ready, TB * i + j + 1)
                for n, (what, jj, c) in enumerate(T_RING):
                    if what != "T" or jj != j:
                        continue
                    pe.wait_ge(t_ready, bank_count(i, n, project))
                    for r in range(4 * c, min(4 * c + 4, j + 1)):
                        mm = pe.transpose(ps_t[:, n % 2, (r - 4 * c) * P:(r - 4 * c + 1) * P],
                                          prob[:, j % 2, r * P:(r + 1) * P], ident[:])
                    mm.then_inc(t_done, 1)

            def pv(i, u, j, project):
                last = max(n for n, (what, jj, _) in enumerate(T_RING) if what == "T" and jj == j)
                pe.wait_ge(t_ready, ring_count(i, last, project))
                pe.wait_ge(o_high, TB * i + j + 1)
                for r in range(j + 1):
                    for n, (a, c) in enumerate(PASSES):
                        mm = pe.matmul(ps_o[:, 0:P], vh[:, u, a, r * D:(r + 1) * D], probT[:, j % 2, c, r * P:(r + 1) * P],
                                       start=(r + n == 0), stop=(r == j and n == 2))
                mm.then_inc(o_done, 1)

            def project_y(i, h, j):
                pe.wait_ge(o_ready, TB * i + j + 1)
                pe.wait_ge(y_added, TB * i + j + 1)
                for n, (a, c) in enumerate(PASSES):
                    mm = pe.matmul(ps_y[:, 0:C], oT[:, j % 2, a, :], wo[:, c, bass.ds(h, 1), :].rearrange("p a c -> p (a c)"),
                                   start=(n == 0), stop=(n == 2))
                mm.then_inc(y_done, 1)

            BEFORE = (-2, -1, 0, 2, 3, 1, 4, 5)

            def scores_free(i, j, project):
                if j == 5 and project:
                    pe.wait_ge(qf_ready, 2 * i + 4)
                else:
                    pe.wait_ge(p_ready, TB * i + BEFORE[j] + 1)

            def step(i, u, j, project, ahead, first=False):
                un = 1 - u
                if j < TB - 1:
                    transposes(i, j + 1, project)
                elif ahead:
                    transposes(i + 1, 0, True)
                def next_v(half):
                    pe.wait_ge(t_ready, bank_count(i, V_RING[half]))
                    project_v((i + 1) % H, half, V_RING[half] % 2)

                if project and j == 0:
                    pe.wait_ge(xT_in, 32 * ((i + 1) // H) + 32)
                    pe.wait_ge(p_ready, TB * i + 2)
                    project_k(un, (i + 1) % H)
                if project and j in (1, 2):
                    next_v(j - 1)
                if j < TB - 3:
                    scores_free(i, j + 3, project)
                    scores(u, j + 3)
                elif ahead:
                    if j == TB - 3:
                        pe.wait_ge(q_ready, 2 * i + 4)
                        pe.wait_ge(k_ready, 2 * i + 4)
                    scores_free(i + 1, j + 3 - TB, True)
                    scores(un, j + 3 - TB)
                if project and j == 1:
                    project_q(i + 1, un, (i + 1) % H)
                pv(i, u, j, project)
                if not first:
                    if j:
                        project_y(i, i % H, j - 1)
                    else:
                        project_y(i - 1, (i - 1) % H, TB - 1)
                if j == TB - 1 and not ahead:
                    project_y(i, i % H, j)

            def attention(i0, heads, last):
                def steps(i, u, lo, hi, project=True, ahead=True):
                    for j in range(lo, hi):
                        step(i, u, j, project, ahead)

                step(i0, 0, 0, True, True, first=True)
                with pe.Fori(i0 // 2, (i0 + heads) // 2 - 1) as ip:
                    steps(2 * ip, 0, 1, TB)
                    steps(2 * ip + 1, 1, 0, TB)
                    steps(2 * ip + 2, 0, 0, 1)
                i = i0 + heads - 2
                steps(i, 0, 1, TB)
                steps(i + 1, 1, 0, TB, project=not last, ahead=False)

            def first_scores(i):
                pe.wait_ge(q_ready, 2 * i + 2)
                pe.wait_ge(k_ready, 2 * i + 2)
                scores(0, 0)
                scores(0, 1)
                pe.wait_ge(p_ready, TB * i + 1)
                scores(0, 2)
                transposes(i, 0, True)

            pe.wait_ge(route_ready, 2)
            pe.wait_ge(xT_in, 32)
            pe.wait_ge(wsplit, 4)
            project_k(0, 0)
            project_v(0, 0, 0)
            project_v(0, 1, 1)
            project_q(0, 0, 0)
            pe.wait_ge(qf_ready, 2)
            first_scores(0)
            attention(0, H, False)

            ex_ps = [[ps_s[:, u, 0:512], ps_s[:, u, 512:1024]] for u in range(2)]
            h_ps = [ps_o, ps_y]
            out_ps = [[ps_s[:, 0, 0:C], ps_s[:, 0, 512:512 + C], ps_s[:, 1, 0:C], ps_s[:, 1, 512:512 + C]],
                      [ps_t[:, 0, 0:C], ps_t[:, 1, 0:C], ps_o[:, 0:C], ps_y[:, 0:C]]]
            pe.wait_ge(y_added, TB * H + 1)
            def experts(g, first):
                for u in range(2):
                    n = 2 * g + u
                    pe.wait_ge(ex_in[u], 16 * (g + 1))
                    if not first:
                        pe.wait_ge(eo_a, 2 * g)
                        pe.wait_ge(eo_d, 2 * g)
                    for e in range(EG):
                        for k in range(KC):
                            mm = pe.transpose(ex_ps[u][e // 2][:, ((e % 2) * KC + k) * P:((e % 2) * KC + k + 1) * P],
                                              ex[:, u, e, k * P:(k + 1) * P], ident[:])
                    mm.then_inc(et_done, 1)
                for u in range(2):
                    n = 2 * g + u
                    pe.wait_ge(eup_in[u], 16 * EG * (g + 1))
                    pe.wait_ge(eta_ready, n + 1)
                    pe.wait_ge(etd_ready, n + 1)
                    for e in range(EG):
                        for k in range(KC):
                            mm = pe.matmul(ps_t[:, u, e * 2 * HE:(e + 1) * 2 * HE], exT[:, u, e, k, :], eup[:, u, e, k, :],
                                           start=(k == 0), stop=(k == KC - 1))
                    mm.then_inc(eu_done, 1)
                for u in range(2):
                    n = 2 * g + u
                    pe.wait_ge(eh_ready, n + 1)
                    pe.transpose(h_ps[u][:, 0:P], eh[:, u, :, :].rearrange("p e h -> p (e h)"), ident[:]).then_inc(eht_done, 1)
                for u in range(2):
                    n = 2 * g + u
                    pe.wait_ge(edn_in[u], 16 * (g + 1))
                    pe.wait_ge(eht_ready, 2 * g + 2)
                    for e in range(EG):
                        mm = pe.matmul(out_ps[u][e], ehT[e * HE:(e + 1) * HE, u, :],
                                       edn[e * HE:(e + 1) * HE, u, :], start=True, stop=True)
                    mm.then_inc(ed_done, 1)

            experts(0, True)
            with pe.Fori(1, E // EG // 2) as g:
                experts(g, False)
            pe.wait_ge(eo_a, E // EG)
            pe.wait_ge(eo_d, E // EG)
            first_scores(H)
            attention(H, (B - 1) * H, True)

        @block.scalar
        def _(act):
            def high_weights(r):
                for n in range(2):
                    w, scale = (wq, wk, wv, wo)[2 * r + n], scales[:, 2 * r + n:2 * r + n + 1]
                    act.wait_ge(wscale_step, 8 * r + 8)
                    if 2 * r + n == 3:
                        act.wait_ge(cvec_done, 1)
                    nc.scalar.activation(w[:, 0, :, :].rearrange("p a b -> p (a b)"), stg[n], ACT.Copy, scale=scale)
                    nc.scalar.activation(stg[n], stg[n], ACT.Copy, scale=scale).then_inc(whigh, 1)

            def copy_xt(g):
                act.wait_ge(xt_done, g + 1)
                for k in range(KC):
                    nc.scalar.copy(xnt[:, k, :], ps_s[:, 0, k * 512:(k + 1) * 512]).then_inc(xt_ready, 1)

            def group(g, before, after):
                if before:
                    act.wait_ge(xt_stored, 32 * g)
                act.wait_ge(xt_ready, KC * g + KC)
                nc.scalar.copy(xnth[:, 0, :, :], xnt[:]).then_inc(xn_high, 1)
                act.wait_ge(z_step, 2 * g + 2)
                for n in range(2):
                    src = ps_s[:, 1, n * 512:n * 512 + 2 * (E + 2 * HS)].rearrange("p (t n) -> p t n", t=2)[:, :, E + HS:]
                    nc.scalar.activation(sg[:, 2 * n:2 * n + 2, :], src, ACT.Exp, scale=-1.0).then_inc(g_exp, 1)
                if after:
                    act.wait_ge(xn_low, KC * g + KC)
                    copy_xt(g + 1)
                act.wait_ge(ht_done, g + 1)
                nc.scalar.copy(hsT[:], ps_t[:, 0, 0:2 * P]).then_inc(ht_ready, 1)

            act.wait_ge(stats_ready, 1)
            nc.scalar.activation(std[:], var[:], ACT.Sqrt).then_inc(std_ready, 1)
            copy_xt(0)
            high_weights(0)
            group(0, False, True)
            high_weights(1)
            with act.Fori(1, NG - 1) as g:
                group(g, True, True)
            group(NG - 1, True, False)
            act.wait_ge(z_read, 2 * NG)
            nc.scalar.activation(wexp[:], v8all[:, :, 0:TOPK], ACT.Exp, scale=-1.0).then_inc(logit_exp, 1)

            def softmax_exp(i, j):
                act.wait_ge(max_ready, TB * i + j + 1)
                w = (j + 1) * P
                nc.scalar.activation(prob[:, j % 2, 0:w], ps_s[:, S_SLOT[j], 0:w], ACT.Exp, bias=nmax[:, j:j + 1],
                                     scale=logit_scale[:], accum_out=rsum[:, j:j + 1]).then_inc(p_ready, 1)

            def high_transposed(i, j, project):
                for n, (what, jj, c) in enumerate(T_RING):
                    if what == "T" and jj == j:
                        act.wait_ge(t_done, ring_count(i, n, project))
                        w = min(4, j + 1 - 4 * c) * P
                        nc.scalar.copy(probT[:, j % 2, 0, 4 * c * P:4 * c * P + w], ps_t[:, n % 2, 0:w]).then_inc(t_high, 1)

            def high_k(i, u, h):
                for half in range(2):
                    act.wait_ge(k_done, 2 * i + half + 1)
                    nc.scalar.copy(hold_a[:, 1 + half:2 + half], logit_scale[:])
                    cols = slice(half * 512, (half + 1) * 512)
                    nc.scalar.activation(kT[:, u, 0, cols], ps_s[:, 1, cols], ACT.Identity, bias=bkT[:, bass.ds(h, 1)]).then_inc(k_high, 1)

            def high_q(i, u):
                act.wait_ge(qf_ready, 2 * i + 2)
                nc.scalar.copy(qT[:, u, 0, :], qf[:]).then_inc(q_high, 1)

            def high_v(done, u, half, bank):
                act.wait_ge(t_done, done)
                nc.scalar.copy(vh[:, u, 0, half * 512:(half + 1) * 512], ps_t[:, bank, :]).then_inc(t_high, 1)

            def step(i, u, j, project, ahead, first=False):
                un = 1 - u
                if j < TB - 1:
                    high_transposed(i, j + 1, project)
                elif ahead:
                    high_transposed(i + 1, 0, True)
                if project and j in (1, 2):
                    high_v(ring_count(i, V_RING[j - 1]), un, j - 1, V_RING[j - 1] % 2)
                if project and j == 0:
                    high_k(i + 1, un, (i + 1) % H)
                if j == 1:
                    softmax_exp(i, 4)
                if 3 <= j < TB - 2:
                    softmax_exp(i, j + 2)
                elif j >= TB - 2 and ahead:
                    softmax_exp(i + 1, j + 2 - TB)
                act.wait_ge(o_done, TB * i + j + 1)
                nc.scalar.activation(oT[:, j % 2, 0, :], ps_o[:, 0:P], ACT.Copy, scale=O_SHIFT)
                nc.scalar.activation(oF[:, j % 2, :], ps_o[:, 0:P], ACT.Copy, scale=O_SHIFT).then_inc(o_high, 1)
                if j == 0:
                    softmax_exp(i, 3)
                if j == TB - 1 and ahead:
                    softmax_exp(i + 1, 2)
                if project and j == 1:
                    high_q(i + 1, un)

            def attention(i0, heads, last):
                def steps(i, u, lo, hi, project=True, ahead=True):
                    for j in range(lo, hi):
                        step(i, u, j, project, ahead)

                step(i0, 0, 0, True, True, first=True)
                with act.Fori(i0 // 2, (i0 + heads) // 2 - 1) as ip:
                    steps(2 * ip, 0, 1, TB)
                    steps(2 * ip + 1, 1, 0, TB)
                    steps(2 * ip + 2, 0, 0, 1)
                i = i0 + heads - 2
                steps(i, 0, 1, TB)
                steps(i + 1, 1, 0, TB, project=not last, ahead=False)

            act.wait_ge(wscale_step, WSTEPS)
            nc.scalar.copy(hold_a[:, 0:1], logit_scale[:]).then_inc(o_high, 1)
            high_k(0, 0, 0)
            high_v(1, 0, 0, 0)
            high_v(2, 0, 1, 1)
            high_q(0, 0)
            softmax_exp(0, 0)
            softmax_exp(0, 1)
            high_transposed(0, 0, True)
            softmax_exp(0, 2)
            attention(0, H, False)

            def experts(g, first):
                for u in range(2):
                    n = 2 * g + u
                    act.wait_ge(et_done, n + 1)
                    nc.scalar.copy(exT[:, u, 0:2, :, :].rearrange("p e k s -> p (e k s)"), ps_s[:, u, 0:512]).then_inc(eta_ready, 1)
                for u in range(2):
                    n = 2 * g + u
                    act.wait_ge(eu_done, n + 1)
                    src = ps_t[:, u, 0:EG * 2 * HE].rearrange("p (e n) -> p e n", e=EG)[:, :, 0:HE]
                    nc.scalar.activation(eg[:, u, :, :], src, ACT.Exp, scale=-1.0).then_inc(eg_exp, 1)
                for u in range(2):
                    n = 2 * g + u
                    act.wait_ge(eht_done, n + 1)
                    nc.scalar.copy(ehT[:, u, :], (ps_o, ps_y)[u][:, 0:P]).then_inc(eht_ready, 1)
                for u in range(2):
                    n = 2 * g + u
                    act.wait_ge(ed_done, n + 1)
                    if not first:
                        act.wait_ge(eo_stored, 32 * g)
                    src = ps_t[:, :, 0:C] if u else ps_s[:, 0, :].rearrange("p (e c) -> p e c", e=2)[:, :, 0:C]
                    nc.scalar.copy(eo[:, u, 0:2, :], src).then_inc(eo_a, 1)
                for u in range(2):
                    n = 2 * g + u
                    act.wait_ge(eo_a, n + 1)
                    act.wait_ge(eo_d, n + 1)
                    dst = eout_d[0:SLOTS, :].rearrange("(g e p) c -> p g e c", e=EG, p=P)
                    act.dma_start(dst[:, bass.ds(n, 1), :, :].rearrange("p a e c -> p (a e) c"), eo[:, u, :, :]).then_inc(eo_stored, 16)

            experts(0, True)
            with act.Fori(1, E // EG // 2) as g:
                experts(g, False)
            softmax_exp(H, 0)
            softmax_exp(H, 1)
            high_transposed(H, 0, True)
            softmax_exp(H, 2)
            attention(H, (B - 1) * H, True)

        @block.vector
        def _(dve):
            V = nc.vector
            dve.wait_ge(x_in, 32)
            for t in range(NT):
                V.bn_stats(stats[:, t, :], resid[:, t, :]).then_inc(ln_step, 1)
            steps = [NT]

            def ln(ins):
                steps[0] += 1
                ins.then_inc(ln_step, 1)
                dve.wait_ge(ln_step, steps[0])

            dve.wait_ge(ln_step, NT)
            me, se, mo, so = stats[:, :, 1], stats[:, :, 2], stats[:, :, 4], stats[:, :, 5]
            ln(V.tensor_tensor(mean[:], me, mo, ALU.add))
            ln(V.tensor_scalar(mean[:], mean[:], 0.5, None, ALU.mult))
            ln(V.tensor_tensor(tmp_a[:], me, mo, ALU.subtract))
            ln(V.tensor_tensor(tmp_a[:], tmp_a[:], tmp_a[:], ALU.mult))
            ln(V.tensor_tensor(tmp_b[:], se, so, ALU.add))
            ln(V.scalar_tensor_tensor(tmp_b[:], tmp_a[:], C / 4.0, tmp_b[:], ALU.mult, ALU.add))
            V.tensor_scalar(var[:], tmp_b[:], 1.0 / C, EPS, ALU.mult, ALU.add).then_inc(stats_ready, 1)
            dve.wait_ge(std_ready, 1)
            ln(V.reciprocal(tmp_a[:], std[:]))
            ln(V.tensor_tensor(tmp_a[:], tmp_a[:], var[:], ALU.mult))
            ln(V.tensor_tensor(tmp_a[:], tmp_a[:], std[:], ALU.add))
            ln(V.tensor_scalar(tmp_a[:], tmp_a[:], 0.5, None, ALU.mult))
            ln(V.reciprocal(std[:], tmp_a[:]))
            dve.wait_ge(w_in, W_IN)
            V.tensor_copy(bvB[:], bvT[:].unsqueeze(2).to_broadcast([P, H, P])).then_inc(bias_ready, 1)
            wcount = [0]

            def wstep(ins):
                wcount[0] += 1
                ins.then_inc(wscale_step, 1)
                dve.wait_ge(wscale_step, wcount[0])

            def weight_scales(r):
                two = slice(2 * r, 2 * r + 2)
                if r == 0:
                    V.tensor_reduce(biasmax[:, 0:1], bqT[:], AX.X, ALU.max, apply_absolute_value=True).then_inc(wmax_step, 1)
                    V.tensor_reduce(biasmax[:, 1:2], bkT[:], AX.X, ALU.max, apply_absolute_value=True).then_inc(wmax_step, 1)
                for n in range(2):
                    dve.wait_ge((wload, wreload)[r][n], 16)
                    V.tensor_reduce(absmax[:, 2 * r + n:2 * r + n + 1], stg[n], AX.X, ALU.max,
                                    apply_absolute_value=True).then_inc(wmax_step, 1)
                dve.wait_ge(wmax_step, 2 * r + 4)
                if r == 0:
                    V.scalar_tensor_tensor(bound[:, two], absmax[:, two], XN_BOUND * XN_BOUND, biasmax[:],
                                           ALU.mult, ALU.add).then_inc(bounds_ready, 1)
                else:
                    wstep(V.tensor_scalar(bound[:, 2:3], absmax[:, 2:3], XN_BOUND * XN_BOUND, None, ALU.mult))
                    V.tensor_copy(bound[:, 3:4], absmax[:, 3:4]).then_inc(bounds_ready, 1)
                dve.wait_ge(scale_ready, r + 1)
                wstep(V.tensor_scalar(expo_u[:, two], bounds[:, two].bitcast(U32), 23, None, ALU.logical_shift_right))
                wstep(V.tensor_copy(expo[:, two], expo_u[:, two]))
                wstep(V.tensor_scalar(expo[:, two], expo[:, two], -1.0, float(TOP + 126 + 127), ALU.mult, ALU.add))
                wstep(V.tensor_scalar(expo[:, two], expo[:, two], 1.0, 253.0, ALU.max, ALU.min))
                wstep(V.tensor_copy(expo_u[:, two], expo[:, two]))
                wstep(V.tensor_scalar(scales[:, two].bitcast(U32), expo_u[:, two], 23, None, ALU.logical_shift_left))
                wstep(V.tensor_scalar(expo[:, two], expo[:, two], -1.0, 254.0, ALU.mult, ALU.add))
                wstep(V.tensor_copy(sinv_u[:, two], expo[:, two]))

            gs = [ps_s[:, 1, n * 512:n * 512 + 2 * (E + 2 * HS)].rearrange("p (t n) -> p t n", t=2) for n in range(2)]

            def normalise(g, before):
                if before:
                    dve.wait_ge(xn_stored, 16 * g)
                    dve.wait_ge(xt_done, g)
                for t in range(G4):
                    V.tensor_scalar(xn[:, t, :], resid[:, bass.ds(g * G4 + t, 1), :].rearrange("p a c -> p (a c)"),
                                    mean[:, bass.ds(g * G4 + t, 1)], std[:, bass.ds(g * G4 + t, 1)],
                                    ALU.subtract, ALU.mult).then_inc(xn_ready, 1)

            def add_shared(g):
                dve.wait_ge(d_done, g + 1)
                for n, src in enumerate((ps_t[:, 1, :], ps_o[:])):
                    dst = resid[:, bass.ds(g * G4, G4), :].rearrange("p (a t) c -> p t a c", t=2)[:, n, :, :]
                    V.tensor_tensor(dst, src.rearrange("p (a c) -> p a c", a=2), dst, ALU.add).then_inc(d_added, 1)

            def group(g, before, after):
                if after:
                    normalise(g + 1, True)
                dve.wait_ge(xn_high, g + 1)
                for k in range(KC):
                    V.tensor_tensor(xnth[:, 1, k, :], xnt[:, k, :], xnth[:, 0, k, :], ALU.subtract).then_inc(xn_low, 1)
                dve.wait_ge(g_done, g + 1)
                for n in range(2):
                    V.tensor_scalar(z[:, 2 * n:2 * n + 2, :], gs[n][:, :, 0:E], LOGIT_LOW, LOGIT_HIGH, ALU.max, ALU.min).then_inc(z_step, 1)
                dve.wait_ge(z_step, 2 * g + 2)
                V.memset(hold_v[:, 0:1], 0.0)
                for t in range(G4):
                    V.max(v8[:, t, :], z[:, t, :]).then_inc(top_step, 1)
                dve.wait_ge(g_exp, 2 * g + 2)
                V.tensor_scalar(sg[:], sg[:], 1.0, None, ALU.add).then_inc(hs_step, 1)
                dve.wait_ge(hs_step, 4 * g + 1)
                V.reciprocal(sh[:], sg[:]).then_inc(hs_step, 1)
                dve.wait_ge(hs_step, 4 * g + 2)
                for n in range(2):
                    V.tensor_tensor(sg[:, 2 * n:2 * n + 2, :], gs[n][:, :, E + HS:], sh[:, 2 * n:2 * n + 2, :], ALU.mult).then_inc(hs_step, 1)
                dve.wait_ge(hs_step, 4 * g + 4)
                for n in range(2):
                    ins = V.tensor_tensor(sh[:, 2 * n:2 * n + 2, :], gs[n][:, :, E:E + HS], sg[:, 2 * n:2 * n + 2, :], ALU.mult)
                ins.then_inc(hs_ready, 1)
                dve.wait_ge(top_step, 2 * G4 * g + G4)
                V.memset(hold_v[:, 1:2], 0.0)
                for t in range(G4):
                    V.max_index(i8[:, t, :], v8[:, t, :], z[:, t, :]).then_inc(top_step, 1)
                V.tensor_copy(v8all[:, bass.ds(g * G4, G4), :], v8[:]).then_inc(z_read, 1)
                dve.wait_ge(top_step, 2 * G4 * g + 2 * G4)
                V.tensor_copy(i8all[:, bass.ds(g * G4, G4), :], i8[:]).then_inc(z_read, 1)
                if before:
                    add_shared(g - 1)

            normalise(0, False)
            dve.wait_ge(w_in, W_IN)
            weight_scales(0)
            group(0, False, True)
            weight_scales(1)
            wstep(V.tensor_scalar(scale_u[:], sinv_u[:], 23, None, ALU.logical_shift_left))
            inv = scale_u[:].bitcast(F32)
            wstep(V.tensor_tensor(logit_scale[:], inv[:, 0:1], inv[:, 1:2], ALU.mult))
            wstep(V.tensor_scalar(logit_scale[:], logit_scale[:], SCALE, None, ALU.mult))
            wstep(V.tensor_tensor(out_scale[:], inv[:, 2:3], inv[:, 3:4], ALU.mult))
            wstep(V.tensor_scalar(out_scale[:], out_scale[:], 1.0 / O_SHIFT, None, ALU.mult))
            wstep(V.tensor_scalar(bqT[:], bqT[:], scales[:, 0:1], None, ALU.mult))
            wstep(V.tensor_scalar(bkT[:], bkT[:], scales[:, 1:2], None, ALU.mult))
            V.memset(hold_v[:, 2:3], 0.0).then_inc(y_added, 1)

            dve.wait_ge(cvec_done, 1)
            V.tensor_tensor(cvec[:], ps_y[:, 0:C], cvec[:], ALU.add).then_inc(cvec_ready, 1)

            with dve.Fori(1, NG - 1) as g:
                group(g, True, True)
            group(NG - 1, True, False)
            add_shared(NG - 1)

            count = [0]

            def step(ins):
                count[0] += 1
                ins.then_inc(route_step, 1)
                dve.wait_ge(route_step, count[0])

            dve.wait_ge(z_read, 2 * NG)
            dve.wait_ge(wsplit, 4)
            dve.wait_ge(const_ready, 5)

            step(V.tensor_copy(i8b[:], i8all[:]))
            step(V.tensor_copy(iota_b16[:], iota_e[:]))
            dve.wait_ge(xn_stored, 16 * NG)
            dve.wait_ge(xt_done, NG)
            chosen = []
            for spare in (got[:].rearrange("p u k c -> p (u k c)"), bvB[:].rearrange("p h c -> p (h c)"),
                          xn[:].rearrange("p t c -> p (t c)")):
                halves = spare.bitcast(BF16)
                for n in range(halves.shape[1] // (NT * E)):
                    chosen.append(halves[:, n * NT * E:(n + 1) * NT * E].rearrange("p (t e) -> p t e", t=NT))
            for k in range(TOPK):
                ins = V.tensor_tensor(chosen[k], iota_b16[:].unsqueeze(1).to_broadcast([P, NT, E]),
                                      i8b[:, :, k:k + 1].to_broadcast([P, NT, E]), ALU.is_equal)
                if k:
                    step(ins)
                    ins = V.tensor_tensor(maskb[:], chosen[0] if k == 1 else maskb[:], chosen[k], ALU.add)
                if k < TOPK - 1:
                    step(ins)
            ins.then_inc(mask_ready, 1)
            dve.wait_ge(count_done, 1)
            totals = (ps_t[:, 0, :], ps_t[:, 1, :], ps_o[:], ps_y[:])
            for n in range(4):
                step(V.tensor_copy(tot_a[:, 8 * n:8 * n + 8, :].rearrange("p t e -> p (t e)"), totals[n]))
            src, dst = tot_a, tot_b
            d = 1
            while d < NT:
                step(V.tensor_copy(dst[:, 0:d, :], src[:, 0:d, :]))
                step(V.tensor_tensor(dst[:, d:, :], src[:, d:, :], src[:, 0:NT - d, :], ALU.add))
                src, dst = dst, src
                d *= 2
            for n in range(4):
                got_n = ps_s[:, n // 2, (n % 2) * 512:(n % 2 + 1) * 512].rearrange("p (t e) -> p t e", t=8)
                lo = 1 if n == 0 else 0
                if n == 0:
                    step(V.tensor_copy(cnt[:, 0:1, :], got_n[:, 0:1, :]))
                step(V.tensor_tensor(cnt[:, 8 * n + lo:8 * n + 8, :], got_n[:, lo:, :], src[:, 8 * n + lo - 1:8 * n + 7, :], ALU.add))
            step(V.tensor_scalar(eq[:], cnt[:], float(CAP), 4.0 * SLOTS, ALU.is_gt, ALU.mult))
            step(V.tensor_tensor(cnt[:], cnt[:], slot0[:].unsqueeze(1).to_broadcast([P, NT, E]), ALU.add))
            step(V.tensor_tensor(cnt[:], cnt[:], eq[:], ALU.add))
            step(V.tensor_scalar(cnt[:], cnt[:], float(SLOTS), None, ALU.min))
            for k in range(TOPK):
                step(V.tensor_tensor(eq[:], chosen[k], cnt[:], ALU.mult))
                step(V.tensor_reduce(slotf[:, :, k:k + 1], eq[:], AX.X, ALU.add))
            V.tensor_copy(slot_idx[:], slotf[:]).then_inc(route_ready, 1)
            dve.wait_ge(logit_exp, 1)
            step(V.tensor_scalar(wexp[:], wexp[:], 1.0, None, ALU.add))
            step(V.reciprocal(slotf[:], wexp[:]))
            step(V.tensor_reduce(wsum[:], slotf[:], AX.X, ALU.add))
            step(V.reciprocal(wsum[:], wsum[:]))
            V.tensor_tensor(gate_w[:], slotf[:], wsum[:].unsqueeze(2).to_broadcast([P, NT, TOPK]), ALU.mult).then_inc(route_ready, 1)

            def full_q(i):
                for half in range(2):
                    dve.wait_ge(q_done, 2 * i + half + 1)
                    slots = slice(half * (H // 2), (half + 1) * (H // 2))
                    V.tensor_tensor(qf[:].rearrange("p (t m) -> p m t", m=H)[:, slots, :],
                                    ps_s[:, 1, half * 512:(half + 1) * 512].rearrange("p (m t) -> p m t", m=H // 2),
                                    bqT[:, slots].unsqueeze(2).to_broadcast([P, H // 2, TPH]), ALU.add).then_inc(qf_ready, 1)

            def low_q(i, u, half):
                dve.wait_ge(q_high, i + 1)
                cols = slice(half * 512, (half + 1) * 512)
                V.tensor_tensor(qT[:, u, 1, cols], qf[:, cols], qT[:, u, 0, cols], ALU.subtract).then_inc(q_ready, 1)

            def low_k(i, u, h):
                for half in range(2):
                    dve.wait_ge(k_high, 2 * i + half + 1)
                    cols = slice(half * 512, (half + 1) * 512)
                    V.scalar_tensor_tensor(kT[:, u, 1, cols], ps_s[:, 1, cols], bkT[:, bass.ds(h, 1)], kT[:, u, 0, cols],
                                           ALU.add, ALU.subtract).then_inc(k_ready, 1)

            def low_v(high, u, half, bank):
                dve.wait_ge(t_high, high)
                part_v = slice(half * 512, (half + 1) * 512)
                V.tensor_tensor(vh[:, u, 1, part_v], ps_t[:, bank, :], vh[:, u, 0, part_v], ALU.subtract).then_inc(t_ready, 1)

            def block_max(i, j):
                dve.wait_ge(s_done, TB * i + j + 1)
                V.tensor_reduce(nmax0[:, j:j + 1], ps_s[:, S_SLOT[j], 0:(j + 1) * P], AX.X, ALU.max, negate=True).then_inc(max_step, 1)
                dve.wait_ge(max_step, TB * i + j + 1)
                V.tensor_tensor(nmax[:, j:j + 1], nmax0[:, j:j + 1], logit_scale[:], ALU.mult).then_inc(max_ready, 1)

            def low_transposed(i, j, project):
                for n, (what, jj, c) in enumerate(T_RING):
                    if what == "T" and jj == j:
                        dve.wait_ge(t_high, ring_count(i, n, project))
                        w = min(4, j + 1 - 4 * c) * P
                        cols = slice(4 * c * P, 4 * c * P + w)
                        V.tensor_tensor(probT[:, j % 2, 1, cols], ps_t[:, n % 2, 0:w], probT[:, j % 2, 0, cols],
                                        ALU.subtract).then_inc(t_ready, 1)

            def invert_sum(i, j):
                dve.wait_ge(p_ready, TB * i + j + 1)
                V.reciprocal(rinv[:, j:j + 1], rsum[:, j:j + 1]).then_inc(r_step, 1)

            def scale_of_y(i, j):
                dve.wait_ge(r_step, TB * i + j + 1)
                V.tensor_tensor(yscale[:, j:j + 1], rinv[:, j:j + 1], out_scale[:], ALU.mult).then_inc(r_ready, 1)

            def add_y(i, b, j):
                dve.wait_ge(y_done, TB * i + j + 1)
                dve.wait_ge(r_ready, TB * i + j + 1)
                row = resid[:, bass.ds(b * TB + j, 1), :].rearrange("p a c -> p (a c)")
                V.scalar_tensor_tensor(out=row, in0=ps_y[:, 0:C], scalar=yscale[:, j:j + 1], in1=row,
                                       op0=ALU.mult, op1=ALU.add).then_inc(y_added, 1)

            def step(i, u, j, project, ahead, first=False):
                un = 1 - u
                ib, jb = (i, j - 1) if j else (i - 1, TB - 1)
                if not first:
                    invert_sum(ib, jb)
                if j < TB - 1:
                    low_transposed(i, j + 1, project)
                elif ahead:
                    low_transposed(i + 1, 0, True)
                if not first:
                    scale_of_y(ib, jb)
                if project and j == 0:
                    low_k(i + 1, un, (i + 1) % H)
                if project and j in (1, 2):
                    low_v(ring_count(i, V_RING[j - 1]), un, j - 1, V_RING[j - 1] % 2)
                if j < TB - 3:
                    block_max(i, j + 3)
                elif ahead:
                    block_max(i + 1, j + 3 - TB)
                if project and j == 1:
                    full_q(i + 1)
                dve.wait_ge(o_high, TB * i + j + 2)
                V.tensor_tensor(oT[:, j % 2, 1, :], oF[:, j % 2, :], oT[:, j % 2, 0, :], ALU.subtract).then_inc(o_ready, 1)
                if not first:
                    add_y(ib, ib // H, jb)
                if project and j in (2, 3):
                    low_q(i + 1, un, j - 2)
                if j == TB - 1 and not ahead:
                    invert_sum(i, j)
                    scale_of_y(i, j)
                    add_y(i, i // H, j)

            def attention(i0, heads, last):
                def steps(i, u, lo, hi, project=True, ahead=True):
                    for j in range(lo, hi):
                        step(i, u, j, project, ahead)

                step(i0, 0, 0, True, True, first=True)
                with dve.Fori(i0 // 2, (i0 + heads) // 2 - 1) as ip:
                    steps(2 * ip, 0, 1, TB)
                    steps(2 * ip + 1, 1, 0, TB)
                    steps(2 * ip + 2, 0, 0, 1)
                i = i0 + heads - 2
                steps(i, 0, 1, TB)
                steps(i + 1, 1, 0, TB, project=not last, ahead=False)

            low_k(0, 0, 0)
            low_v(1, 0, 0, 0)
            low_v(2, 0, 1, 1)
            full_q(0)
            low_q(0, 0, 0)
            low_q(0, 0, 1)
            block_max(0, 0)
            block_max(0, 1)
            block_max(0, 2)
            low_transposed(0, 0, True)
            attention(0, H, False)

            def experts(g, first):
                for u in range(2):
                    n = 2 * g + u
                    dve.wait_ge(et_done, n + 1)
                    V.tensor_copy(exT[:, u, 2:4, :, :].rearrange("p e k s -> p (e k s)"), ps_s[:, u, 512:1024]).then_inc(etd_ready, 1)
                for u in range(2):
                    n = 2 * g + u
                    up = ps_t[:, u, 0:EG * 2 * HE].rearrange("p (e n) -> p e n", e=EG)
                    dve.wait_ge(eg_exp, n + 1)
                    V.tensor_scalar(eg[:, u], eg[:, u], 1.0, None, ALU.add).then_inc(eh_step, 1)
                    dve.wait_ge(eh_step, 3 * n + 1)
                    V.reciprocal(eh[:, u], eg[:, u]).then_inc(eh_step, 1)
                    dve.wait_ge(eh_step, 3 * n + 2)
                    V.tensor_tensor(eg[:, u], up[:, :, 0:HE], eh[:, u], ALU.mult).then_inc(eh_step, 1)
                    dve.wait_ge(eh_step, 3 * n + 3)
                    V.tensor_tensor(eh[:, u], up[:, :, HE:], eg[:, u], ALU.mult).then_inc(eh_ready, 1)
                for u in range(2):
                    n = 2 * g + u
                    dve.wait_ge(ed_done, n + 1)
                    if not first:
                        dve.wait_ge(eo_stored, 32 * g)
                    if u:
                        V.tensor_copy(eo[:, u, 2, :], ps_o[:, 0:C])
                        V.tensor_copy(eo[:, u, 3, :], ps_y[:, 0:C]).then_inc(eo_d, 1)
                    else:
                        V.tensor_copy(eo[:, u, 2:4, :], ps_s[:, 1, :].rearrange("p (e c) -> p e c", e=2)[:, :, 0:C]).then_inc(eo_d, 1)

            experts(0, True)
            with dve.Fori(1, E // EG // 2) as g:
                experts(g, False)
            block_max(H, 0)
            block_max(H, 1)
            block_max(H, 2)
            low_transposed(H, 0, True)
            attention(H, (B - 1) * H, True)
            dve.wait_ge(routed_in, 16 * B)
            dve.wait_ge(y_added, TB * B * H + 1)
            dve.wait_ge(fin_ready, B - 1)
            tiles = resid[:, (B - 1) * TB:, :]
            V.tensor_tensor(tiles, tiles, got[:].rearrange("p u k c -> p (u k) c")[:, 0:TB, :], ALU.add).then_inc(fin_ready, 1)


_INS = ["L0_attn_x", "L0_attn_Wq", "L0_attn_bq", "L0_attn_Wk", "L0_attn_bk", "L0_attn_Wv", "L0_attn_bv", "L0_attn_Wo",
        "L0_attn_bo", "L0_ffn_w_gate", "L0_ffn_w_shared_up", "L0_ffn_w_shared_down", "L0_ffn_w_up", "L0_ffn_w_down"]


def kernel(**inputs):
    import numpy as _np
    import concourse.bacc as _bacc
    from concourse import mybir as _mybir
    from concourse.bass_utils import run_bass_kernel_spmd as _run

    nc = _bacc.Bacc("TRN2", target_bir_lowering=False, num_devices=1)
    arrays, args = {}, []
    for name in _INS:
        a = _np.ascontiguousarray(inputs[name])
        arrays[f"in_{name}_dram"] = a
        args.append(nc.dram_tensor(f"in_{name}_dram", a.shape, _mybir.dt.from_np(a.dtype), kind="ExternalInput").ap())
    shape = inputs["L0_attn_x"].shape
    args.append(nc.dram_tensor("out_0_dram", shape, _mybir.dt.from_np(_np.dtype("float32")), kind="ExternalOutput").ap())
    causal_attention_with_moe(nc, *args)
    r = _run(nc, [arrays], core_ids=[0])
    return r.results[0]["out_0_dram"]
```
